# Optimizing a Trainium2 kernel written in Bass

```python
import numpy as np
import jax
import jax.numpy as jnp

def _softmax(x, axis=-1):
    return jax.nn.softmax(x, axis=axis)

def _gelu(x):
    return jax.nn.gelu(x, approximate=True)

def _silu(x):
    return jax.nn.silu(x)

def _sigmoid(x):
    return jax.nn.sigmoid(x)

def _layernorm(x, axis=-1, eps=1e-05):
    m = jnp.mean(x, axis=axis, keepdims=True)
    v = jnp.var(x, axis=axis, keepdims=True)
    return (x - m) / jnp.sqrt(v + eps)

def _scatter_add(tgt, idx, src, axis=0):
    return tgt.at[idx].add(src)

def _segment_sum(src, seg, n):
    return jax.ops.segment_sum(src, seg, n)
kernel_name = 'mk_xattn_ffn_d1_seqx_r4_7722c1'

def setup_inputs(seed: int=0):
    np.random.seed(seed)
    _w = jnp.asarray

    def _rec_inputs():
        import jax
        import jax.numpy as jnp
        _rk = jax.random.key(seed)
        x = -0.0003929 + 0.9999 * jax.random.normal(jax.random.fold_in(_rk, 1), (32, 128, 256), jnp.float32)
        _lenS = 128 - jax.random.randint(jax.random.fold_in(_rk, 7), (32,), 0, max(1, 128 // 4) + 1, jnp.int32)
        _lenS2 = 128 - jax.random.randint(jax.random.fold_in(_rk, 8), (32,), 0, max(1, 128 // 4) + 1, jnp.int32)
        _ctx_512P = jax.random.normal(jax.random.fold_in(_rk, 11), (32, 16, 128), jnp.float32)
        _ctx_512c = jax.random.dirichlet(jax.random.fold_in(_rk, 511), 0.3 * jnp.ones((16,), jnp.float32), (32, 128))
        _ctx_512t = jnp.einsum('bsk,bkd->bsd', _ctx_512c, _ctx_512P)
        _ctx_512t = _ctx_512t * jax.lax.rsqrt(jnp.mean(jnp.square(_ctx_512t)) + 1e-12) * 0.953939
        ctx_512 = -1.39393e-06 + 0.999914 * (_ctx_512t + 0.3 * jax.random.normal(jax.random.fold_in(_rk, 611), (32, 128, 128), jnp.float32))
        return (x, ctx_512)
    x, ctx_512 = _rec_inputs()

    def _L0_xattn_setup():
        import jax, jax.numpy as jnp
        import numpy as np
        HEADS = 16
        D_MODEL = 256
        IMG_MODEL = 128
        D_K = D_MODEL // HEADS
        key = jax.random.key(seed)
        ks = jax.random.split(key, 12)
        B, LQ, LKV = (8, 512, 256)
        s_dm = 1.0 / np.sqrt(D_MODEL)
        s_im = 1.0 / np.sqrt(IMG_MODEL)
        return {'q': jax.random.normal(ks[0], (B, LQ, D_MODEL), jnp.float32), 'k': jax.random.normal(ks[1], (B, LKV, IMG_MODEL), jnp.float32), 'v': jax.random.normal(ks[2], (B, LKV, IMG_MODEL), jnp.float32), 'Wq': jax.random.normal(ks[3], (D_MODEL, D_MODEL), jnp.float32) * s_dm, 'bq': jnp.zeros((D_MODEL,), jnp.float32), 'Wk': jax.random.normal(ks[4], (IMG_MODEL, D_MODEL), jnp.float32) * s_im, 'bk': jnp.zeros((D_MODEL,), jnp.float32), 'Wv': jax.random.normal(ks[5], (IMG_MODEL, D_MODEL), jnp.float32) * s_im, 'bv': jnp.zeros((D_MODEL,), jnp.float32), 'Wo': jax.random.normal(ks[6], (D_MODEL, D_MODEL), jnp.float32) * s_dm, 'bo': jnp.zeros((D_MODEL,), jnp.float32)}
    _L0_xattn_all = _L0_xattn_setup()
    _L0_xattn_in = {k: v for k, v in _L0_xattn_all.items() if k in ('Wq', 'bq', 'Wk', 'bk', 'Wv', 'bv', 'Wo', 'bo')}
    del _L0_xattn_all

    def _L0_ffn_setup():
        import jax, jax.numpy as jnp
        import numpy as np
        BEST_K = 2

        def _expert(xf, w1, w3, w2):
            return jax.nn.silu(xf @ w1) * (xf @ w3) @ w2
        key = jax.random.key(seed)
        ks = jax.random.split(key, 9)
        E, S_sh, D, H = (8, 2, 256, 128)
        B, S = (2, 512)
        w = lambda k, shape: jax.random.normal(k, shape, dtype=jnp.float32) * 0.02
        return {'x': jax.random.normal(ks[0], (B, S, D), dtype=jnp.float32), 'router_w': w(ks[1], (D, E)), 'router_b': jnp.zeros((E,), dtype=jnp.float32), 'routed_w1': w(ks[2], (E, D, H)), 'routed_w3': w(ks[3], (E, D, H)), 'routed_w2': w(ks[4], (E, H, D)), 'shared_w1': w(ks[5], (S_sh, D, H)), 'shared_w3': w(ks[6], (S_sh, D, H)), 'shared_w2': w(ks[7], (S_sh, H, D))}
    _L0_ffn_all = _L0_ffn_setup()
    _L0_ffn_in = {k: v for k, v in _L0_ffn_all.items() if k in ('router_w', 'router_b', 'routed_w1', 'routed_w3', 'routed_w2', 'shared_w1', 'shared_w3', 'shared_w2')}
    del _L0_ffn_all
    return {'x': x, 'ctx_512': ctx_512, 'L0_xattn_Wq': _L0_xattn_in['Wq'], 'L0_xattn_bq': _L0_xattn_in['bq'], 'L0_xattn_Wk': _L0_xattn_in['Wk'], 'L0_xattn_bk': _L0_xattn_in['bk'], 'L0_xattn_Wv': _L0_xattn_in['Wv'], 'L0_xattn_bv': _L0_xattn_in['bv'], 'L0_xattn_Wo': _L0_xattn_in['Wo'], 'L0_xattn_bo': _L0_xattn_in['bo'], 'L0_ffn_router_w': _L0_ffn_in['router_w'], 'L0_ffn_router_b': _L0_ffn_in['router_b'], 'L0_ffn_routed_w1': _L0_ffn_in['routed_w1'], 'L0_ffn_routed_w3': _L0_ffn_in['routed_w3'], 'L0_ffn_routed_w2': _L0_ffn_in['routed_w2'], 'L0_ffn_shared_w1': _L0_ffn_in['shared_w1'], 'L0_ffn_shared_w3': _L0_ffn_in['shared_w3'], 'L0_ffn_shared_w2': _L0_ffn_in['shared_w2']}

def reference(x, ctx_512, L0_xattn_Wq, L0_xattn_bq, L0_xattn_Wk, L0_xattn_bk, L0_xattn_Wv, L0_xattn_bv, L0_xattn_Wo, L0_xattn_bo, L0_ffn_router_w, L0_ffn_router_b, L0_ffn_routed_w1, L0_ffn_routed_w3, L0_ffn_routed_w2, L0_ffn_shared_w1, L0_ffn_shared_w3, L0_ffn_shared_w2):
    import jax
    import jax.numpy as jnp

    def _L0_xattn_ref(q, k, v, Wq, bq, Wk, bk, Wv, bv, Wo, bo):
        import jax, jax.numpy as jnp
        import numpy as np
        HEADS = 16
        D_MODEL = 256
        IMG_MODEL = 128
        D_K = D_MODEL // HEADS
        B, LQ, _ = q.shape
        LKV = k.shape[1]
        qh = (q @ Wq + bq).reshape(B, LQ, HEADS, D_K).transpose(0, 2, 1, 3)
        kh = (k @ Wk + bk).reshape(B, LKV, HEADS, D_K).transpose(0, 2, 1, 3)
        vh = (v @ Wv + bv).reshape(B, LKV, HEADS, D_K).transpose(0, 2, 1, 3)
        scale = 1.0 / np.sqrt(D_K)
        scores = jnp.einsum('bhqd,bhkd->bhqk', qh, kh) * scale
        attn = jax.nn.softmax(scores, axis=-1)
        out = jnp.einsum('bhqk,bhkd->bhqd', attn, vh)
        concat = out.transpose(0, 2, 1, 3).reshape(B, LQ, D_MODEL)
        return concat @ Wo + bo

    def _L0_ffn_ref(x, router_w, router_b, routed_w1, routed_w3, routed_w2, shared_w1, shared_w3, shared_w2):
        import jax, jax.numpy as jnp
        import numpy as np
        BEST_K = 2

        def _expert(xf, w1, w3, w2):
            return jax.nn.silu(xf @ w1) * (xf @ w3) @ w2
        B, S, D = x.shape
        T = B * S
        xf = x.reshape(T, D)
        logits = xf @ router_w + router_b
        topk_vals, topk_idx = jax.lax.top_k(logits, BEST_K)
        sparse = jnp.full_like(logits, -jnp.inf)
        sparse = sparse.at[jnp.arange(T)[:, None], topk_idx].set(topk_vals)
        gates = jax.nn.softmax(sparse, axis=-1)
        routed = jax.vmap(_expert, in_axes=(None, 0, 0, 0))(xf, routed_w1, routed_w3, routed_w2)
        routed_out = jnp.einsum('etd,te->td', routed, gates)
        shared_out = jax.vmap(_expert, in_axes=(None, 0, 0, 0))(xf, shared_w1, shared_w3, shared_w2).sum(axis=0)
        return (routed_out + shared_out).reshape(B, S, D)
    x = x + _L0_xattn_ref(_layernorm(x, axis=-1), ctx_512, ctx_512, L0_xattn_Wq, L0_xattn_bq, L0_xattn_Wk, L0_xattn_bk, L0_xattn_Wv, L0_xattn_bv, L0_xattn_Wo, L0_xattn_bo)
    x = x + _L0_ffn_ref(_layernorm(x, axis=-1), L0_ffn_router_w, L0_ffn_router_b, L0_ffn_routed_w1, L0_ffn_routed_w3, L0_ffn_routed_w2, L0_ffn_shared_w1, L0_ffn_shared_w3, L0_ffn_shared_w2)
    return x

_drawn_inputs = setup_inputs


def setup_inputs(seed=0):
    import zlib

    import numpy as np

    out = dict(_drawn_inputs(seed))
    spreads = {'L0_xattn_bq': (0.0, 0.372),
     'L0_xattn_bk': (0.0, 0.8),
     'L0_xattn_bv': (0.0, 0.1),
     'L0_xattn_bo': (0.0, 0.1),
     'L0_ffn_router_b': (0.0, 0.8)}
    factors = {'L0_ffn_router_w': 8.0,
     'L0_ffn_routed_w1': 7.75,
     'L0_ffn_routed_w3': 7.672,
     'L0_ffn_routed_w2': 7.668,
     'L0_ffn_shared_w1': 3.927,
     'L0_ffn_shared_w3': 3.867,
     'L0_ffn_shared_w2': 3.866}
    for name, (base, spread) in spreads.items():
        noise = np.random.default_rng([zlib.crc32(name.encode()), seed]).standard_normal(out[name].shape)
        drawn = base * np.exp(spread * noise) if base else spread * noise
        out[name] = jnp.asarray(drawn.astype(out[name].dtype))
    for name, factor in factors.items():
        out[name] = (out[name] * factor).astype(out[name].dtype)
    return out
```

```python
from contextlib import ExitStack

import concourse.bass as bass
from concourse import mybir

F32 = mybir.dt.float32
F32R = mybir.dt.float32r
BF16 = mybir.dt.bfloat16
ALU = mybir.AluOpType
ACT = mybir.ActivationFunctionType
AX = mybir.AxisListType

NB, T, D = 32, 128, 256
DC = 128
H, DK = 16, 16
E_SH, E_RT, HID = 2, 8, 128
NE = E_SH + E_RT
B = 4
G = NB // B
TG = B * T
C = D // 128
HC = 128 // DK
NQ = H // 4
EPS = 1e-5
PARTS = 3
Q_PART = [0, 0, 0, 1, 1, 2]
K_PART = [0, 1, 2, 0, 1, 0]
KD = len(Q_PART) * DK
KM = KD + PARTS

WQ = 0
WK = WQ + C * D
WV = WK + D
WO = WV + D
RW = WO + C * D
ATT_W = RW + C * E_RT
W1 = ATT_W
W3 = W1 + NE * C * HID
W2 = W3 + NE * C * HID
ALL_W = W2 + NE * D
FFN_W = NE * C * HID

STAGE_COLS = [(0, ATT_W), (W1, W3), (W3, W2), (W2, ALL_W)]
STAGE_COUNT = [5 * 16, 9 * 16, 13 * 16, 15 * 16]
CONST_DMAS = 8
CONSTS = 6

FRONT_USES = ["xT0", "xT1", "cT", "Q0", "Q1", "K0", "K1", "V01", "V23"]
FRONT_BANK = [0, 1, 0, 1, 0, 1, 0, 1, 0]


def build(nc, x, ctx_in, Wq, bq, Wk, bk, Wv, bv, Wo, bo, rw, rb, rw1, rw3, rw2, sw1, sw3, sw2,
          ident_in, before_in, out):
    with ExitStack() as stack:
        def sb(name, shape, dt=F32):
            return stack.enter_context(nc.sbuf_tensor(name, shape, dt))

        def pb(name, shape=(128, 512), dt=F32):
            return stack.enter_context(nc.psum_tensor(name, list(shape), dt))

        def sem(name):
            return stack.enter_context(nc.semaphore(name))

        w_hi = sb("w_hi", [128, ALL_W], F32R)
        w_lo = sb("w_lo", [128, ALL_W], F32R)
        ffn_f32 = sb("ffn_f32", [128, FFN_W])
        acc = ffn_f32[:, 0:B * D].rearrange("p (b d) -> p b d", b=B)
        gate_act = ffn_f32[:, B * D:B * D + TG]
        hidden = [ffn_f32[:, B * D + (1 + i) * TG:B * D + (2 + i) * TG] for i in range(2)]
        stage = ffn_f32

        x_in = sb("x_in", [128, B, D])
        x_res = sb("x_res", [128, B, D])
        xn = sb("xn", [128, B, D])
        x2 = sb("x2", [128, B, D])
        xn2 = sb("xn2", [128, B, D])
        c_in = sb("c_in", [128, B, DC])
        xnT_hi = sb("xnT_hi", [128, C, TG], F32R)
        xnT_lo = sb("xnT_lo", [128, C, TG], F32R)
        cT_hi = sb("cT_hi", [128, TG], F32R)
        cT_lo = sb("cT_lo", [128, TG], F32R)
        xn2T_hi = sb("xn2T_hi", [128, C, TG], F32R)
        xn2T_lo = sb("xn2T_lo", [128, C, TG], F32R)
        proj = sb("proj", [128, 2, TG])
        rest = sb("rest", [128, 2, TG])
        parts = sb("parts", [128, 2, PARTS, C, TG], BF16)
        q_stack = sb("q_stack", [128, H, TG], BF16)
        k_stack = sb("k_stack", [128, H, TG], BF16)
        v_aug = sb("v_aug", [128, B, H, DK + 1])
        prob = [sb(f"prob{i}", [128, 4 * T]) for i in range(2)]
        cat = sb("cat", [128, D])
        catT_hi = sb("catT_hi", [128, C, T], F32R)
        catT_lo = sb("catT_lo", [128, C, T], F32R)
        hid_hi = [sb(f"hid_hi{i}", [128, TG], F32R) for i in range(2)]
        hid_lo = [sb(f"hid_lo{i}", [128, TG], F32R) for i in range(2)]
        stats = sb("stats", [128, B, 6])
        mean_parts = sb("mean_parts", [128, 3, B])
        mean = sb("mean", [128, B])
        var_eps = sb("var_eps", [128, B])
        rstd = sb("rstd", [128, B])
        stats2 = sb("stats2", [128, B, 6])
        mv2 = sb("mv2", [128, B, 2])
        var_eps2 = sb("var_eps2", [128, B])
        rstd2 = sb("rstd2", [128, B])
        row_max = sb("row_max", [128, B, H])
        max_rest = sb("max_rest", [128, B, H])
        neg_max = sb("neg_max", [128, B, 128], BF16)
        neg_maxT = sb("neg_maxT", [128, B, T], BF16)
        rden = sb("rden", [128, H])
        logits = sb("logits", [128, B, E_RT])
        pair_gt = sb("pair_gt", [128, B, E_RT, E_RT])
        pair_ge = sb("pair_ge", [128, B, E_RT, E_RT])
        rank = sb("rank", [128, B, E_RT])
        chosen = sb("chosen", [128, B, E_RT])
        top = sb("top", [128, B])
        shifted = sb("shifted", [128, B, E_RT])
        expo = sb("expo", [128, B, E_RT])
        gsum = sb("gsum", [128, B])
        grec = sb("grec", [128, B])
        gates = sb("gates", [128, B, E_RT])
        ident = sb("ident", [128, 128])
        ident_b = sb("ident_b", [128, 128], BF16)
        before = sb("before", [128, E_RT, E_RT])
        minus_half = sb("minus_half", [128, B])
        bo_rep = sb("bo_rep", [128, D])
        bv_rep = sb("bv_rep", [128, 2, D])
        rb_rep = sb("rb_rep", [128, E_RT])
        bq_col = sb("bq_col", [128, C])
        bq_quarter = sb("bq_quarter", [128, C])
        bk_col = sb("bk_col", [128, C])

        parts_dram = nc.dram_tensor("parts_dram", [2, PARTS, C, 128, TG], BF16, kind="Internal").ap()
        nm_dram = nc.dram_tensor("nm_dram", [B, PARTS * H, T], BF16, kind="Internal").ap()

        misc = [pb("misc0"), pb("misc1")]
        s_bank = pb("s_bank")
        st_bank = [pb("st_bank0"), pb("st_bank1")]
        h1_bank = pb("h1_bank")
        h3_bank = pb("h3_bank")
        y_bank = pb("y_bank")

        consts_in = sem("consts_in")
        stage_in = sem("stage_in")
        stage_hi = sem("stage_hi")
        stage_lo = sem("stage_lo")
        const_ready = sem("const_ready")
        x_loaded = sem("x_loaded")
        c_loaded = sem("c_loaded")
        var_ready = sem("var_ready")
        rstd_ready = sem("rstd_ready")
        xn_ready = sem("xn_ready")
        res_ready = sem("res_ready")
        front_full = sem("front_full")
        front_hi = sem("front_hi")
        front_lo = sem("front_lo")
        proj_ready = sem("proj_ready")
        part1_ready = sem("part1_ready")
        rest_ready = sem("rest_ready")
        part2_ready = sem("part2_ready")
        part3_ready = sem("part3_ready")
        v_ready = sem("v_ready")
        parts_out = sem("parts_out")
        stack_in = sem("stack_in")
        s_full = sem("s_full")
        s_max = sem("s_max")
        nm_ready = sem("nm_ready")
        nmT_full = sem("nmT_full")
        nmT_ready = sem("nmT_ready")
        nm_out = sem("nm_out")
        nm_in = [sem(f"nm_in{b}") for b in range(B)]
        st_full = [sem(f"st_full{i}") for i in range(2)]
        exp_done = [sem(f"exp_done{i}") for i in range(2)]
        pv_done = [sem(f"pv_done{i}") for i in range(2)]
        cat_ready = sem("cat_ready")
        catT_full = sem("catT_full")
        catT_hi_done = sem("catT_hi_done")
        catT_lo_done = sem("catT_lo_done")
        wo_full = sem("wo_full")
        x2_ready = sem("x2_ready")
        var2_ready = sem("var2_ready")
        rstd2_ready = sem("rstd2_ready")
        xn2_ready = sem("xn2_ready")
        dve_att = sem("dve_att")
        dve_ffn = sem("dve_ffn")
        xn2T_full = sem("xn2T_full")
        xn2T_hi_done = sem("xn2T_hi_done")
        xn2T_lo_done = sem("xn2T_lo_done")
        logits_full = sem("logits_full")
        logits_out = sem("logits_out")
        shifted_ready = sem("shifted_ready")
        expo_ready = sem("expo_ready")
        h1_full = sem("h1_full")
        h3_full = sem("h3_full")
        tanh_done = sem("tanh_done")
        u_done = sem("u_done")
        v_done = sem("v_done")
        hid_hi_done = sem("hid_hi_done")
        hid_lo_done = sem("hid_lo_done")
        y_full = sem("y_full")
        acc_done = sem("acc_done")
        gates_step = sem("gates_step")
        out_done = sem("out_done")

        FRONT = 9
        XT0, XT1, CT, Q0, Q1, K0, K1, V01, V23 = range(FRONT)
        DVE_ATT = 33
        DVE_FFN = 8
        Y_USES = 2 * NE

        def wait_if(eng, g, semaphore, value, before_first=False):
            if not (isinstance(g, int) and g == 0):
                eng.wait_ge(semaphore, value)

        SLOTS = NE
        S_SLOT, NMT_SLOT, ST_SLOT, WO_SLOT = 2, 3, 4, 5

        def in_slot(s, first):
            return s - first if 0 <= s - first < B else None

        def in_groups(eng, body):
            body(0, None)
            with eng.Fori(1, G) as g:
                body(g, g - 1)
            body(None, G - 1)

        block = stack.enter_context(nc.Block())

        @block.sync
        def _(sp):
            def rep(ap_1d, n):
                return ap_1d.rearrange("(a n) -> a n", a=1).broadcast_to([128, n])

            def load_x(first):
                sp.dma_start(x_in[:], x[bass.ds(first, B)].rearrange("b p d -> p b d")).then_inc(x_loaded, 16)

            def load_c(first):
                sp.dma_start(c_in[:], ctx_in[bass.ds(first, B)].rearrange("b p d -> p b d")).then_inc(c_loaded, 16)

            sp.dma_start(x_in[:], x[0:B].rearrange("b p d -> p b d")).then_inc(x_loaded, 16)
            sp.dma_start(ident[:], ident_in).then_inc(consts_in, 16)
            sp.dma_start(c_in[:], ctx_in[0:B].rearrange("b p d -> p b d")).then_inc(c_loaded, 16)
            for cols, src in ((slice(WQ, WK), Wq.rearrange("(c p) n -> p c n", c=C)),
                              (slice(WO, RW), Wo.rearrange("(c p) n -> p c n", c=C)),
                              (slice(RW, ATT_W), rw.rearrange("(c p) n -> p c n", c=C))):
                sp.dma_start(stage[:, cols].rearrange("p (c n) -> p c n", c=C), src).then_inc(stage_in, 16)
            sp.dma_start(stage[:, WK:WV], Wk).then_inc(stage_in, 16)
            sp.dma_start(stage[:, WV:WO], Wv).then_inc(stage_in, 16)
            sp.dma_start(bq_col[:], bq.rearrange("(c p) -> p c", c=C), allow_slow_non_contiguous=True).then_inc(consts_in, 16)
            sp.dma_start(bk_col[:], bk.rearrange("(c p) -> p c", c=C), allow_slow_non_contiguous=True).then_inc(consts_in, 16)
            sp.dma_start(bo_rep[:], rep(bo, D)).then_inc(consts_in, 16)
            sp.dma_start(bv_rep[:, 0, :], rep(bv, D)).then_inc(consts_in, 16)
            sp.dma_start(bv_rep[:, 1, :], rep(bv, D)).then_inc(consts_in, 16)
            sp.dma_start(rb_rep[:], rep(rb, E_RT)).then_inc(consts_in, 16)
            sp.dma_start(before[:], before_in).then_inc(consts_in, 16)

            def store(g, first):
                sp.wait_ge(acc_done, (g + 1) * (NE * B))
                sp.dma_start(out[bass.ds(first, B)].rearrange("b p d -> p b d"), acc).then_inc(out_done, 16)

            def load_stage(n):
                sp.wait_ge(stage_hi, n)
                sp.wait_ge(stage_lo, n)
                shared, routed, width = ((sw1, rw1, C * HID), (sw3, rw3, C * HID), (sw2, rw2, D))[n - 1]
                for src, lo, hi in ((shared, 0, E_SH), (routed, E_SH, NE)):
                    dst = stage[:, lo * width:hi * width]
                    if n < 3:
                        for c in range(C):
                            sp.dma_start(dst.rearrange("p (e c h) -> p e c h", c=C, h=HID)[:, :, c, :],
                                         src[:, c * 128:(c + 1) * 128, :].rearrange("e p h -> p e h")).then_inc(stage_in, 16)
                    else:
                        sp.dma_start(dst.rearrange("p (e d) -> p e d", d=D),
                                     src.rearrange("e h d -> h e d")).then_inc(stage_in, 16)

            def body(ga, gf):
                if ga is not None:
                    load_from = ga * B if isinstance(ga, int) else sp.snap(ga * B)
                if gf is not None:
                    store_to = (gf - 1) * B if isinstance(gf, int) else sp.snap((gf - 1) * B)
                if not (isinstance(ga, int) and ga == 0) and ga is not None:
                    sp.wait_ge(xn_ready, ga * B)
                    sp.wait_ge(res_ready, ga)
                    load_x(load_from)
                    sp.wait_ge(front_full, (ga - 1) * FRONT + CT + 1)
                    load_c(load_from)
                if gf is not None and not (isinstance(gf, int) and gf == 0):
                    store(gf - 1, store_to)
                if ga is not None:
                    for side in range(2):
                        sp.wait_ge(part3_ready, ga * 4 + 2 * side + 2)
                        sp.dma_start(parts_dram[side].rearrange("s c p t -> p (s c) t"),
                                     parts[:, side].rearrange("p s c t -> p (s c) t")).then_inc(parts_out, 16)
                        sp.wait_ge(parts_out, ga * 32 + 16 * side + 16)
                        for j, s in enumerate((Q_PART, K_PART)[side]):
                            dst = (q_stack, k_stack)[side][j * DK:(j + 1) * DK, :, :]
                            sp.dma_start(dst, parts_dram[side, s].rearrange("c (h d) t -> d (c h) t", d=DK)).then_inc(stack_in, 16)
                for s in range(SLOTS):
                    if ga is not None:
                        if gf is None and s in (0, 3, 6):
                            load_stage(s // 3 + 1)
                        b = in_slot(s, NMT_SLOT)
                        if b is not None:
                            sp.wait_ge(nmT_ready, ga * B + b + 1)
                            sp.dma_start(nm_dram[b], neg_maxT[0:PARTS * H, b, :]).then_inc(nm_out, 16)
                            sp.wait_ge(nm_out, (ga * B + b + 1) * 16)
                            sp.dma_start(q_stack[KD:KM, :, b * T:(b + 1) * T],
                                         nm_dram[b].rearrange("(s h) t -> s h t", s=PARTS)).then_inc(nm_in[b], 16)

            body(0, None)
            body(1, 0)
            with sp.Fori(2, G) as g:
                body(g, g - 1)
            body(None, G - 1)
            store(G - 1, (G - 1) * B)
            sp.wait_ge(out_done, G * 16)

        @block.gpsimd
        def _(pool):
            pool.memset(minus_half[:], -0.5).then_inc(const_ready, 1)
            pool.wait_ge(consts_in, CONST_DMAS * 16)

            def body(ga, gf):
                if ga is not None:
                    pool.wait_ge(var_ready, ga + 1)
                    if isinstance(ga, int) and ga == 0:
                        pool.wait_ge(const_ready, CONSTS)
                    pool.tensor_tensor(rstd[:], var_eps[:], minus_half[:], ALU.pow).then_inc(rstd_ready, 1)
                    pool.wait_ge(x_loaded, (ga + 1) * 16)
                    wait_if(pool, ga, x2_ready, ga * B)
                    pool.tensor_tensor(x_res[:], x_in[:], bo_rep[:].unsqueeze(1).broadcast_to([128, B, D]),
                                       ALU.add).then_inc(res_ready, 1)
                    for n in range(4):
                        pool.wait_ge(part2_ready, ga * 4 + n + 1)
                        side, m = divmod(n, 2)
                        wait_if(pool, ga, parts_out, ga * 32)
                        pool.tensor_tensor(parts[:, side, 2, m, :], rest[:, n % 2, :], parts[:, side, 1, m, :],
                                           ALU.subtract).then_inc(part3_ready, 1)
                for s in range(SLOTS):
                    if gf is not None:
                        pool.wait_ge(v_done, gf * NE + s + 1)
                        pool.wait_ge(hid_hi_done, gf * NE + s + 1)
                        pool.tensor_tensor(hid_lo[s % 2][:], hidden[s % 2], hid_hi[s % 2][:].bitcast(F32),
                                           ALU.subtract).then_inc(hid_lo_done, 1)
                    b = in_slot(s, WO_SLOT)
                    if ga is not None and b is not None:
                        pool.wait_ge(var2_ready, ga * B + b + 1)
                        pool.tensor_tensor(rstd2[:, b:b + 1], var_eps2[:, b:b + 1], minus_half[:, 0:1],
                                           ALU.pow).then_inc(rstd2_ready, 1)
            in_groups(pool, body)

        @block.scalar
        def _(act):
            def split_stage(n):
                act.wait_ge(stage_in, STAGE_COUNT[n])
                lo, hi = STAGE_COLS[n]
                act.activation(w_hi[:, lo:hi], stage[:, 0:hi - lo], ACT.Copy).then_inc(stage_hi, 1)

            act.wait_ge(const_ready, CONSTS)
            split_stage(0)

            def body(ga, gf):
                if ga is not None:
                    for use, dst in ((XT0, xnT_hi[:, 0, :]), (XT1, xnT_hi[:, 1, :]), (CT, cT_hi[:])):
                        act.wait_ge(front_full, ga * FRONT + use + 1)
                        act.activation(dst, misc[FRONT_BANK[use]][:], ACT.Copy).then_inc(front_hi, 1)
                    for n, use in enumerate((Q0, Q1, K0, K1)):
                        side, m = divmod(n, 2)
                        act.wait_ge(front_full, ga * FRONT + use + 1)
                        if n >= 2:
                            act.wait_ge(part3_ready, ga * 4 + n - 1)
                        bias = (bq_quarter, bk_col)[side][:, m:m + 1]
                        act.activation(proj[:, n % 2, :], misc[FRONT_BANK[use]][:], ACT.Identity, bias=bias,
                                       scale=(DK ** -0.5, 1.0)[side]).then_inc(proj_ready, 1)
                        act.wait_ge(proj_ready, ga * 4 + n + 1)
                        wait_if(act, ga, parts_out, ga * 32)
                        act.activation(parts[:, side, 0, m, :], proj[:, n % 2, :], ACT.Copy).then_inc(part1_ready, 1)
                        act.wait_ge(rest_ready, ga * 4 + n + 1)
                        act.activation(parts[:, side, 1, m, :], rest[:, n % 2, :], ACT.Copy).then_inc(part2_ready, 1)
                if gf is not None:
                    for c in range(C):
                        act.wait_ge(xn2T_full, gf * C + c + 1)
                        act.activation(xn2T_hi[:, c, :], (h1_bank, h3_bank)[c][:], ACT.Copy).then_inc(xn2T_hi_done, 1)
                for s in range(SLOTS):
                    if ga is not None:
                        b = in_slot(s, WO_SLOT)
                        if b is not None:
                            act.wait_ge(catT_full, ga * B + b + 1)
                            act.activation(catT_hi[:], misc[1][:, 0:C * T].rearrange("p (c t) -> p c t", c=C),
                                           ACT.Copy).then_inc(catT_hi_done, 1)
                    if gf is not None:
                        act.wait_ge(h1_full, gf * NE + s + 1)
                        if s:
                            act.wait_ge(v_done, gf * NE + s)
                        act.activation(gate_act, h1_bank[:], ACT.Tanh, scale=0.5).then_inc(tanh_done, 1)
                        if s == 0:
                            act.wait_ge(shifted_ready, gf + 1)
                            act.activation(expo[:], shifted[:], ACT.Exp).then_inc(expo_ready, 1)
                    if ga is not None:
                        b = in_slot(s, NMT_SLOT)
                        if b is not None:
                            act.wait_ge(nmT_full, ga * B + b + 1)
                            act.activation(neg_maxT[0:PARTS * H, b, :], misc[1][0:PARTS * H, 0:T // 2].bitcast(BF16),
                                           ACT.Copy).then_inc(nmT_ready, 1)
                    for q in range(NQ):
                        b = in_slot(s, ST_SLOT)
                        if ga is not None and b is not None:
                            k, use = q % 2, b * (NQ // 2) + q // 2
                            act.wait_ge(st_full[k], ga * (B * NQ // 2) + use + 1)
                            if use:
                                act.wait_ge(pv_done[k], ga * (B * NQ // 2) + use)
                            act.activation(prob[k][:], st_bank[k][:], ACT.Exp).then_inc(exp_done[k], 1)
                        if q == 0 and gf is not None:
                            act.wait_ge(v_done, gf * NE + s + 1)
                            act.activation(hid_hi[s % 2][:], hidden[s % 2], ACT.Copy).then_inc(hid_hi_done, 1)
                    if gf is None and s in (1, 4, 7):
                        split_stage(s // 3 + 1)
            in_groups(act, body)

        @block.vector
        def _(dve):
            dve.memset(v_aug[:, :, :, DK:DK + 1], 1.0).then_inc(const_ready, 1)
            dve.memset(k_stack[KD:128, :, :], 1.0).then_inc(const_ready, 1)
            dve.memset(neg_max[:], 0.0).then_inc(const_ready, 1)
            dve.wait_ge(consts_in, CONST_DMAS * 16)
            dve.tensor_copy(ident_b[:], ident[:]).then_inc(const_ready, 1)
            dve.tensor_scalar(bq_quarter[:], bq_col[:], DK ** -0.5, None, ALU.mult).then_inc(const_ready, 1)

            def split_stage(n):
                dve.wait_ge(stage_hi, n + 1)
                lo, hi = STAGE_COLS[n]
                dve.tensor_tensor(w_lo[:, lo:hi], stage[:, 0:hi - lo], w_hi[:, lo:hi].bitcast(F32),
                                  ALU.subtract).then_inc(stage_lo, 1)

            def normalised(dst, src, b, mean_of, r):
                return dve.tensor_scalar(dst[:, b, :], src[:, b, :], mean_of, r[:, b:b + 1],
                                         ALU.subtract, ALU.mult)

            def body(ga, gf):
                steps = {"att": 0, "ffn": 0}

                def att_step(ins):
                    steps["att"] += 1
                    ins.then_inc(dve_att, 1)
                    dve.wait_ge(dve_att, ga * DVE_ATT + steps["att"])

                def ffn_step(ins):
                    steps["ffn"] += 1
                    ins.then_inc(dve_ffn, 1)
                    dve.wait_ge(dve_ffn, gf * DVE_FFN + steps["ffn"])

                if ga is not None:
                    dve.wait_ge(x_loaded, (ga + 1) * 16)
                    wait_if(dve, ga, xn_ready, ga * B)
                    for b in range(B):
                        ins = dve.bn_stats(stats[:, b, :], x_in[:, b, :])
                        if b < B - 1:
                            ins.then_inc(dve_att, 1)
                            steps["att"] += 1
                    att_step(ins)
                    even, odd = stats[:, :, 0:3], stats[:, :, 3:6]
                    dve.tensor_tensor(mean_parts[:, 0, :], even[:, :, 1], odd[:, :, 1], ALU.add).then_inc(dve_att, 1)
                    dve.tensor_tensor(mean_parts[:, 1, :], even[:, :, 1], odd[:, :, 1], ALU.subtract).then_inc(dve_att, 1)
                    dve.scalar_tensor_tensor(out=mean_parts[:, 2, :], in0=even[:, :, 2], scalar=D * EPS,
                                             in1=odd[:, :, 2], op0=ALU.add, op1=ALU.add).then_inc(dve_att, 1)
                    steps["att"] += 3
                    dve.wait_ge(dve_att, ga * DVE_ATT + steps["att"])
                    att_step(dve.scalar_tensor_tensor(out=mean_parts[:, 1, :], in0=mean_parts[:, 1, :], scalar=0.25,
                                                      in1=mean_parts[:, 1, :], op0=ALU.mult, op1=ALU.mult))
                    dve.scalar_tensor_tensor(out=var_eps[:], in0=mean_parts[:, 2, :], scalar=1.0 / D,
                                             in1=mean_parts[:, 1, :], op0=ALU.mult, op1=ALU.add).then_inc(var_ready, 1)
                    att_step(dve.tensor_scalar(mean[:], mean_parts[:, 0, :], 0.5, None, ALU.mult))
                    dve.wait_ge(rstd_ready, ga + 1)
                    wait_if(dve, ga, front_full, ga * FRONT)
                    for b in range(B):
                        normalised(xn, x_in, b, mean[:, b:b + 1], rstd).then_inc(xn_ready, 1)
                    if isinstance(ga, int) and ga == 0:
                        split_stage(0)
                    for n, (use, hi, lo) in enumerate(((XT0, xnT_hi[:, 0, :], xnT_lo[:, 0, :]),
                                                       (XT1, xnT_hi[:, 1, :], xnT_lo[:, 1, :]),
                                                       (CT, cT_hi[:], cT_lo[:]))):
                        dve.wait_ge(front_hi, ga * 3 + n + 1)
                        dve.tensor_tensor(lo, misc[FRONT_BANK[use]][:], hi.bitcast(F32),
                                          ALU.subtract).then_inc(front_lo, 1)
                    for n in range(4):
                        side, m = divmod(n, 2)
                        dve.wait_ge(part1_ready, ga * 4 + n + 1)
                        if n >= 2:
                            dve.wait_ge(part3_ready, ga * 4 + n - 1)
                        else:
                            wait_if(dve, ga, part3_ready, ga * 4)
                        dve.tensor_tensor(rest[:, n % 2, :], proj[:, n % 2, :], parts[:, side, 0, m, :],
                                          ALU.subtract).then_inc(rest_ready, 1)
                    for n, use in enumerate((V01, V23)):
                        dve.wait_ge(front_full, ga * FRONT + use + 1)
                        dve.tensor_tensor(v_aug[:, 2 * n:2 * n + 2, :, 0:DK].rearrange("p b h d -> p (b h) d"),
                                          misc[FRONT_BANK[use]][:].rearrange("p (r d) -> p r d", d=DK),
                                          bv_rep[:].rearrange("p b (h d) -> p (b h) d", d=DK),
                                          ALU.add).then_inc(v_ready, 1)
                if gf is not None:
                    for c in range(C):
                        dve.wait_ge(xn2T_hi_done, gf * C + c + 1)
                        dve.tensor_tensor(xn2T_lo[:, c, :], (h1_bank, h3_bank)[c][:], xn2T_hi[:, c, :].bitcast(F32),
                                          ALU.subtract).then_inc(xn2T_lo_done, 1)
                    dve.wait_ge(logits_full, gf + 1)
                    dve.tensor_tensor(logits[:], y_bank[:, 0:B * E_RT].rearrange("p (b e) -> p b e", b=B),
                                      rb_rep[:].unsqueeze(1).broadcast_to([128, B, E_RT]), ALU.add).then_inc(logits_out, 1)
                    dve.wait_ge(logits_out, gf + 1)
                    other = logits[:].unsqueeze(2).broadcast_to([128, B, E_RT, E_RT])
                    own = logits[:].unsqueeze(3).broadcast_to([128, B, E_RT, E_RT])
                    ffn_step(dve.tensor_reduce(top[:], logits[:], AX.X, ALU.max))
                    dve.tensor_tensor(shifted[:], logits[:], top[:].unsqueeze(2).broadcast_to([128, B, E_RT]),
                                      ALU.subtract).then_inc(shifted_ready, 1)
                    dve.wait_ge(shifted_ready, gf + 1)
                    ffn_step(dve.tensor_tensor(pair_ge[:], other, own, ALU.is_ge))
                    ffn_step(dve.tensor_tensor(pair_ge[:], pair_ge[:], before[:].unsqueeze(1).broadcast_to(
                        [128, B, E_RT, E_RT]), ALU.mult))
                    ffn_step(dve.tensor_tensor(pair_gt[:], other, own, ALU.is_gt))
                    ffn_step(dve.tensor_tensor(pair_gt[:], pair_gt[:], pair_ge[:], ALU.max))
                    ffn_step(dve.tensor_reduce(rank[:], pair_gt[:], AX.X, ALU.add))
                for s in range(SLOTS):
                    bs, bt, bw = in_slot(s, S_SLOT), in_slot(s, ST_SLOT), in_slot(s, WO_SLOT)
                    if ga is None:
                        bs = bt = bw = None
                    if bw is not None:
                        dve.wait_ge(catT_hi_done, ga * B + bw + 1)
                        dve.tensor_tensor(catT_lo[:], misc[1][:, 0:C * T].rearrange("p (c t) -> p c t", c=C),
                                          catT_hi[:].bitcast(F32), ALU.subtract).then_inc(catT_lo_done, 1)
                    if gf is not None:
                        dve.wait_ge(tanh_done, gf * NE + s + 1)
                        dve.scalar_tensor_tensor(out=gate_act, in0=gate_act, scalar=1.0, in1=h1_bank[:],
                                                 op0=ALU.add, op1=ALU.mult).then_inc(u_done, 1)
                    if bw is not None:
                        dve.wait_ge(wo_full, ga * B + bw + 1)
                        dve.wait_ge(res_ready, ga + 1)
                        if gf is not None:
                            dve.wait_ge(acc_done, gf * (NE * B) + B)
                        dve.tensor_tensor(x2[:, bw, :], misc[0][:, 0:D], x_res[:, bw, :], ALU.add).then_inc(x2_ready, 1)
                        dve.wait_ge(x2_ready, ga * B + bw + 1)
                        att_step(dve.bn_stats(stats2[:, bw, :], x2[:, bw, :]))
                    for q in range(NQ):
                        if bs is not None:
                            dve.wait_ge(s_full, (ga * B + bs) * NQ + q + 1)
                            dve.tensor_reduce(row_max[:, bs, 4 * q:4 * q + 4],
                                              s_bank[:].rearrange("p (h t) -> p h t", h=4), AX.X,
                                              ALU.max).then_inc(s_max, 1)
                        if gf is not None and q == 0:
                            dve.wait_ge(u_done, gf * NE + s + 1)
                            dve.wait_ge(h3_full, gf * NE + s + 1)
                            if s >= 2:
                                dve.wait_ge(hid_lo_done, gf * NE + s - 1)
                            dve.scalar_tensor_tensor(out=hidden[s % 2], in0=gate_act, scalar=0.5, in1=h3_bank[:],
                                                     op0=ALU.mult, op1=ALU.mult).then_inc(v_done, 1)
                        if bw is not None and q == 0:
                            att_step(dve.bn_aggr(mv2[:, bw, :], stats2[:, bw, :]))
                            dve.tensor_scalar(var_eps2[:, bw:bw + 1], mv2[:, bw, 1:2], EPS, None,
                                              ALU.add).then_inc(var2_ready, 1)
                        if gf is not None and q == 0:
                            if s == 0:
                                dve.wait_ge(expo_ready, gf + 1)
                                ffn_step(dve.scalar_tensor_tensor(out=chosen[:], in0=rank[:], scalar=1.5, in1=expo[:],
                                                                  op0=ALU.is_lt, op1=ALU.mult))
                                ffn_step(dve.tensor_reduce(gsum[:], chosen[:], AX.X, ALU.add))
                                dve.reciprocal(grec[:], gsum[:]).then_inc(gates_step, 1)
                                dve.wait_ge(gates_step, gf * 2 + 1)
                                dve.tensor_tensor(gates[:], chosen[:], grec[:].unsqueeze(2).broadcast_to(
                                    [128, B, E_RT]), ALU.mult).then_inc(gates_step, 1)
                        if gf is not None and s and q in (1, 3):
                            accumulate(dve, gf, s - 1, q - 1)
                            accumulate(dve, gf, s - 1, q)
                    if bs is not None:
                        nm = [neg_max[:, bs, p * H:(p + 1) * H] for p in range(PARTS)]
                        dve.wait_ge(s_max, (ga * B + bs + 1) * NQ)
                        wait_if(dve, ga, nmT_full, ga * B)
                        att_step(dve.tensor_scalar(nm[0], row_max[:, bs, :], -1.0, None, ALU.mult))
                        att_step(dve.scalar_tensor_tensor(out=max_rest[:, bs, :], in0=row_max[:, bs, :], scalar=-1.0,
                                                          in1=nm[0], op0=ALU.mult, op1=ALU.subtract))
                        att_step(dve.tensor_copy(nm[1], max_rest[:, bs, :]))
                        dve.tensor_tensor(nm[2], max_rest[:, bs, :], nm[1], ALU.subtract).then_inc(nm_ready, 1)
                    if bw is not None:
                        dve.wait_ge(rstd2_ready, ga * B + bw + 1)
                        if gf is not None:
                            dve.wait_ge(xn2T_full, (gf + 1) * C)
                        normalised(xn2, x2, bw, mv2[:, bw, 0:1], rstd2).then_inc(xn2_ready, 1)
                    if bt is not None:
                        dve.wait_ge(pv_done[1], (ga * B + bt + 1) * (NQ // 2))
                        pv = misc[0][:, 0:H * (DK + 1)].rearrange("p (h d) -> p h d", h=H)
                        att_step(dve.reciprocal(rden[:], pv[:, :, DK]))
                        if bt:
                            dve.wait_ge(catT_full, ga * B + bt)
                        else:
                            wait_if(dve, ga, catT_full, ga * B)
                        dve.tensor_tensor(cat[:].rearrange("p (h d) -> p h d", h=H), pv[:, :, 0:DK],
                                          rden[:].unsqueeze(2).broadcast_to([128, H, DK]),
                                          ALU.mult).then_inc(cat_ready, 1)
                    if gf is None and s in (1, 4, 7):
                        split_stage(s // 3 + 1)
                if gf is not None:
                    for q in range(B):
                        accumulate(dve, gf, NE - 1, q)
                assert ga is None or steps["att"] == DVE_ATT, steps
                assert gf is None or steps["ffn"] == DVE_FFN, steps

            def accumulate(dve, gf, s, b):
                dve.wait_ge(y_full, gf * Y_USES + 2 * s + b // 2 + 1)
                y = y_bank[:, (b % 2) * D:(b % 2 + 1) * D]
                if s == 0:
                    if b == 0:
                        wait_if(dve, gf, out_done, gf * 16)
                        dve.wait_ge(xn2_ready, (gf + 1) * B)
                    ins = dve.tensor_tensor(acc[:, b, :], y, x2[:, b, :], ALU.add)
                elif s < E_SH:
                    dve.wait_ge(acc_done, (gf * NE + s - 1) * B + b + 1)
                    ins = dve.tensor_tensor(acc[:, b, :], y, acc[:, b, :], ALU.add)
                else:
                    dve.wait_ge(gates_step, gf * 2 + 2)
                    dve.wait_ge(acc_done, (gf * NE + s - 1) * B + b + 1)
                    ins = dve.scalar_tensor_tensor(out=acc[:, b, :], in0=y, scalar=gates[:, b, s - E_SH:s - E_SH + 1],
                                                   in1=acc[:, b, :], op0=ALU.mult, op1=ALU.add)
                ins.then_inc(acc_done, 1)

            in_groups(dve, body)

        @block.tensor
        def _(pe):
            def three(out_ap, terms):
                n = len(terms)
                for i, (lh, ll, rh, rl) in enumerate(terms):
                    pe.matmul(out_ap, lh, rh, start=(i == 0), stop=False)
                    pe.matmul(out_ap, ll, rh, start=False, stop=False)
                    ins = pe.matmul(out_ap, lh, rl, start=False, stop=(i == n - 1))
                return ins

            def weights(start, size):
                return w_hi[:, start:start + size], w_lo[:, start:start + size]

            pe.wait_ge(const_ready, CONSTS)
            pe.wait_ge(consts_in, CONST_DMAS * 16)

            def front_bank_free(ga, use):
                if use == XT0:
                    wait_if(pe, ga, x2_ready, ga * B)
                elif use == XT1:
                    wait_if(pe, ga, catT_lo_done, ga * B)
                elif use in (CT, Q0):
                    pe.wait_ge(front_lo, ga * 3 + use - 1)
                elif use == Q1:
                    pe.wait_ge(front_lo, ga * 3 + 3)
                elif use in (K0, K1):
                    pe.wait_ge(proj_ready, ga * 4 + use - K0 + 1)
                elif use in (V01, V23):
                    pe.wait_ge(proj_ready, ga * 4 + use - V01 + 3)

            def body(ga, gf):
                if ga is not None:
                    for use in (XT0, XT1):
                        front_bank_free(ga, use)
                        for b in range(B):
                            pe.wait_ge(xn_ready, ga * B + b + 1)
                            ins = pe.transpose(misc[FRONT_BANK[use]][:, b * T:(b + 1) * T],
                                               xn[:, b, use * 128:(use + 1) * 128], ident[:])
                        ins.then_inc(front_full, 1)
                    front_bank_free(ga, CT)
                    pe.wait_ge(c_loaded, (ga + 1) * 16)
                    for b in range(B):
                        ins = pe.transpose(misc[FRONT_BANK[CT]][:, b * T:(b + 1) * T], c_in[:, b, :], ident[:])
                    ins.then_inc(front_full, 1)
                    if isinstance(ga, int) and ga == 0:
                        pe.wait_ge(stage_lo, 1)
                    for m in range(C):
                        front_bank_free(ga, Q0 + m)
                        pe.wait_ge(front_lo, ga * 3 + 2)
                        three(misc[FRONT_BANK[Q0 + m]][:],
                              [(*weights(WQ + c * D + m * 128, 128), xnT_hi[:, c, :], xnT_lo[:, c, :]) for c in range(C)]
                              ).then_inc(front_full, 1)
                    pe.wait_ge(front_lo, ga * 3 + 3)
                    for m in range(C):
                        front_bank_free(ga, K0 + m)
                        three(misc[FRONT_BANK[K0 + m]][:],
                              [(*weights(WK + m * 128, 128), cT_hi[:], cT_lo[:])]).then_inc(front_full, 1)
                    for n in range(2):
                        front_bank_free(ga, V01 + n)
                        for b in (2 * n, 2 * n + 1):
                            tok = slice(b * T, (b + 1) * T)
                            ins = three(misc[FRONT_BANK[V01 + n]][:, (b % 2) * D:(b % 2 + 1) * D],
                                        [(cT_hi[:, tok], cT_lo[:, tok], *weights(WV, D))])
                        ins.then_inc(front_full, 1)
                if gf is not None:
                    for c in range(C):
                        for b in range(B):
                            pe.wait_ge(xn2_ready, gf * B + b + 1)
                            if c == 0 and b == 0:
                                wait_if(pe, gf, v_done, gf * NE)
                            ins = pe.transpose((h1_bank, h3_bank)[c][:, b * T:(b + 1) * T],
                                               xn2[:, b, c * 128:(c + 1) * 128], ident[:])
                        ins.then_inc(xn2T_full, 1)
                    pe.wait_ge(xn2T_lo_done, (gf + 1) * C)
                    wait_if(pe, gf, acc_done, gf * (NE * B))
                    for b in range(B):
                        tok = slice(b * T, (b + 1) * T)
                        ins = three(y_bank[:, b * E_RT:(b + 1) * E_RT],
                                    [(xn2T_hi[:, c, tok], xn2T_lo[:, c, tok], *weights(RW + c * E_RT, E_RT))
                                     for c in range(C)])
                    ins.then_inc(logits_full, 1)

                def up(which, s):
                    bank, start = ((h1_bank, W1), (h3_bank, W3))[which]
                    if s == 0 and which == 0:
                        pe.wait_ge(stage_lo, 4)
                    if s:
                        pe.wait_ge((u_done, v_done)[which], gf * NE + s)
                    three(bank[:], [(*weights(start + (s * C + c) * HID, HID), xn2T_hi[:, c, :], xn2T_lo[:, c, :])
                                    for c in range(C)]).then_inc((h1_full, h3_full)[which], 1)

                def down(s, half):
                    k = s % 2
                    pe.wait_ge(hid_lo_done, gf * NE + s + 1)
                    if s == 0 and half == 0:
                        pe.wait_ge(logits_out, gf + 1)
                    else:
                        pe.wait_ge(acc_done, gf * (NE * B) + s * B + 2 * half)
                    for b in (2 * half, 2 * half + 1):
                        tok = slice(b * T, (b + 1) * T)
                        ins = three(y_bank[:, (b % 2) * D:(b % 2 + 1) * D],
                                    [(hid_hi[k][:, tok], hid_lo[k][:, tok], *weights(W2 + s * D, D))])
                    ins.then_inc(y_full, 1)

                def scores(b, q):
                    if b == 0 and q == 0:
                        pe.wait_ge(stack_in, (ga + 1) * (12 * 16))
                    if b or q:
                        pe.wait_ge(s_max, (ga * B + b) * NQ + q)
                    else:
                        wait_if(pe, ga, s_max, ga * (B * NQ))
                    tok = slice(b * T, (b + 1) * T)
                    for j in range(4):
                        ins = pe.matmul(s_bank[:, j * T:(j + 1) * T], q_stack[0:KD, 4 * q + j, tok],
                                        k_stack[0:KD, 4 * q + j, tok], start=True, stop=True)
                    ins.then_inc(s_full, 1)

                def scores_t(b, q):
                    k, use = q % 2, b * (NQ // 2) + q // 2
                    if q == 0:
                        pe.wait_ge(nm_in[b], (ga + 1) * 16)
                    if use:
                        pe.wait_ge(exp_done[k], ga * (B * NQ // 2) + use)
                    else:
                        wait_if(pe, ga, exp_done[k], ga * (B * NQ // 2))
                    tok = slice(b * T, (b + 1) * T)
                    for j in range(4):
                        ins = pe.matmul(st_bank[k][:, j * T:(j + 1) * T], k_stack[0:KM, 4 * q + j, tok],
                                        q_stack[0:KM, 4 * q + j, tok], start=True, stop=True)
                    ins.then_inc(st_full[k], 1)

                def values(b, q):
                    k, use = q % 2, b * (NQ // 2) + q // 2
                    pe.wait_ge(exp_done[k], ga * (B * NQ // 2) + use + 1)
                    if q == 0:
                        pe.wait_ge(v_ready, (ga + 1) * 2)
                        if b:
                            pe.wait_ge(x2_ready, ga * B + b)
                    for j in range(4):
                        h = 4 * q + j
                        ins = pe.matmul(misc[0][:, h * (DK + 1):(h + 1) * (DK + 1)], prob[k][:, j * T:(j + 1) * T],
                                        v_aug[:, b, h, :], start=True, stop=True)
                    ins.then_inc(pv_done[k], 1)

                for s in range(SLOTS):
                    if ga is not None:
                        b = in_slot(s, WO_SLOT)
                        if b is not None:
                            pe.wait_ge(cat_ready, ga * B + b + 1)
                            pe.wait_ge(nmT_ready, ga * B + min(b + 2, B))
                            for c in range(C):
                                ins = pe.transpose(misc[1][:, c * T:(c + 1) * T], cat[:, c * 128:(c + 1) * 128], ident[:])
                            ins.then_inc(catT_full, 1)
                    if gf is not None:
                        up(0, s)
                    if ga is not None:
                        b = in_slot(s, WO_SLOT)
                        if b is not None:
                            pe.wait_ge(catT_lo_done, ga * B + b + 1)
                            three(misc[0][:, 0:D], [(catT_hi[:, c, :], catT_lo[:, c, :], *weights(WO + c * D, D))
                                                    for c in range(C)]).then_inc(wo_full, 1)
                        b = in_slot(s, NMT_SLOT)
                        if b is not None:
                            pe.wait_ge(nm_ready, ga * B + b + 1)
                            if b >= 2:
                                pe.wait_ge(catT_lo_done, ga * B + b - 1)
                            elif b == 0:
                                pe.wait_ge(v_ready, ga * 2 + 1)
                            else:
                                pe.wait_ge(nmT_ready, ga * B + b)
                            pe.transpose(misc[1][:, 0:T // 2].bitcast(BF16), neg_max[:, b, :],
                                         ident_b[:]).then_inc(nmT_full, 1)
                    bs, bt = in_slot(s, S_SLOT), in_slot(s, ST_SLOT)
                    for q in range(NQ):
                        if ga is not None and bs is not None:
                            scores(bs, q)
                        if ga is not None and bt is not None:
                            scores_t(bt, q)
                            if q:
                                values(bt, q - 1)
                        if gf is not None:
                            if q == 0:
                                up(1, s)
                            elif q in (1, 3) and s:
                                down(s - 1, q // 2)
                    if ga is not None and bt is not None:
                        values(bt, NQ - 1)
                if gf is not None:
                    down(NE - 1, 0)
                    down(NE - 1, 1)
            in_groups(pe, body)



_INS = ["x", "ctx_512", "L0_xattn_Wq", "L0_xattn_bq", "L0_xattn_Wk", "L0_xattn_bk", "L0_xattn_Wv", "L0_xattn_bv",
        "L0_xattn_Wo", "L0_xattn_bo", "L0_ffn_router_w", "L0_ffn_router_b", "L0_ffn_routed_w1", "L0_ffn_routed_w3",
        "L0_ffn_routed_w2", "L0_ffn_shared_w1", "L0_ffn_shared_w3", "L0_ffn_shared_w2"]


def kernel(**inputs):
    import numpy as np
    import concourse.bacc as bacc
    from concourse import mybir as mb
    from concourse.bass_utils import run_bass_kernel_spmd as run

    nc = bacc.Bacc("TRN2", target_bir_lowering=False, num_devices=1)
    arrays, args = {}, []
    given = [(name, np.ascontiguousarray(inputs[name])) for name in _INS]
    given.append(("identity", np.eye(128, dtype=np.float32)))
    lower = np.tri(E_RT, E_RT, -1, dtype=np.float32)
    given.append(("before", np.ascontiguousarray(np.broadcast_to(lower, (128, E_RT, E_RT)))))
    for name, a in given:
        arrays[f"in_{name}"] = a
        args.append(nc.dram_tensor(f"in_{name}", a.shape, mb.dt.from_np(a.dtype), kind="ExternalInput").ap())
    args.append(nc.dram_tensor("out_x", (NB, T, D), F32, kind="ExternalOutput").ap())
    build(nc, *args)
    r = run(nc, [arrays], core_ids=[0])
    return r.results[0]["out_x"]
```

```python
from contextlib import ExitStack

import concourse.bass as bass
from concourse import mybir

F32 = mybir.dt.float32
F32R = mybir.dt.float32r
BF16 = mybir.dt.bfloat16
ALU = mybir.AluOpType
ACT = mybir.ActivationFunctionType
AX = mybir.AxisListType

NB, T, D = 32, 128, 256
DC = 128
H, DK = 16, 16
E_SH, E_RT, HID = 2, 8, 128
NE = E_SH + E_RT
B = 4
G = NB // B
TG = B * T
C = D // 128
HC = 128 // DK
NQ = H // 4
EPS = 1e-5
PARTS = 3
Q_PART = [0, 0, 0, 1, 1, 2]
K_PART = [0, 1, 2, 0, 1, 0]
KD = len(Q_PART) * DK
KM = KD + PARTS
VW = 32

WQ = 0
WK = WQ + C * D
WV = WK + D
WO = WV + D
RW = WO + C * D
ATT_W = RW + C * E_RT
W1 = ATT_W
W3 = W1 + NE * C * HID
W2 = W3 + NE * C * HID
ALL_W = W2 + NE * D
FFN_W = NE * C * HID

STAGE_COLS = [(0, ATT_W), (W1, W3), (W3, W2), (W2, ALL_W)]
STAGE_COUNT = [5 * 16, 9 * 16, 13 * 16, 15 * 16]

FRONT = 9
CT, XT0, XT1, K0, K1, Q0, Q1, V01, V23 = range(FRONT)
FRONT_PE = {(4, 1): CT, (5, 0): XT0, (5, 2): XT1, (6, 0): K0, (6, 2): K1, (7, 0): Q0, (7, 2): Q1, (8, 0): V01, (8, 2): V23}
SPLIT_T = {(4, 2): 0, (5, 1): 1, (5, 3): 2}
FIRST_PART = {(6, 1): 0, (6, 3): 1, (7, 1): 2, (7, 3): 3}
OTHER_PARTS = {(6, 3): 0, (7, 1): 1, (7, 3): 2, (8, 1): 3}
TAKE_V = {(8, 1): 0, (8, 3): 1}
TURN = (8, 3)
SPARE_Y = 7
S_SLOT, NMT_SLOT, ST_SLOT, WO_SLOT = 0, 1, 2, 3


def build(nc, x, ctx_in, Wq, bq, Wk, bk, Wv, bv, Wo, bo, rw, rb, rw1, rw3, rw2, sw1, sw3, sw2,
          ident_in, before_in, out):
    with ExitStack() as stack:
        def sb(name, shape, dt=F32):
            return stack.enter_context(nc.sbuf_tensor(name, shape, dt))

        def pb(name, shape=(128, 512), dt=F32):
            return stack.enter_context(nc.psum_tensor(name, list(shape), dt))

        def sem(name):
            return stack.enter_context(nc.semaphore(name))

        w_hi = sb("w_hi", [128, ALL_W], F32R)
        w_lo = sb("w_lo", [128, ALL_W], F32R)
        ffn_f32 = sb("ffn_f32", [128, FFN_W])
        acc = ffn_f32[:, 0:B * D].rearrange("p (b d) -> p b d", b=B)
        gate_act = ffn_f32[:, B * D:B * D + TG]
        hidden = [ffn_f32[:, B * D + (1 + i) * TG:B * D + (2 + i) * TG] for i in range(2)]
        stage = ffn_f32

        x_in = sb("x_in", [128, B, D])
        x_res = sb("x_res", [128, B, D])
        xn = sb("xn", [128, B, D])
        x2 = sb("x2", [128, B, D])
        xn2 = sb("xn2", [128, B, D])
        c_in = sb("c_in", [128, B, DC])
        xnT_hi = sb("xnT_hi", [128, C, TG], F32R)
        xnT_lo = sb("xnT_lo", [128, C, TG], F32R)
        cT_hi = sb("cT_hi", [128, TG], F32R)
        cT_lo = sb("cT_lo", [128, TG], F32R)
        xn2T_hi = sb("xn2T_hi", [128, C, TG], F32R)
        xn2T_lo = sb("xn2T_lo", [128, C, TG], F32R)
        proj = sb("proj", [128, 2, TG])
        parts = sb("parts", [128, 2, PARTS, C, TG], BF16)
        q_stack = sb("q_stack", [128, H, TG], BF16)
        k_stack = sb("k_stack", [128, H, TG], BF16)
        v_aug = sb("v_aug", [128, B, H, VW])
        outT = sb("outT", [128, NQ * T])
        prob = [sb(f"prob{i}", [128, 4 * T]) for i in range(2)]
        cat = sb("cat", [128, D])
        catT_hi = sb("catT_hi", [128, C, T], F32R)
        catT_lo = sb("catT_lo", [128, C, T], F32R)
        hid_hi = [sb(f"hid_hi{i}", [128, TG], F32R) for i in range(2)]
        hid_lo = [sb(f"hid_lo{i}", [128, TG], F32R) for i in range(2)]
        stats = sb("stats", [128, B, 6])
        mean_parts = sb("mean_parts", [128, 3, B])
        mean = sb("mean", [128, B])
        var_eps = sb("var_eps", [128, B])
        rstd = sb("rstd", [128, B])
        stats2 = sb("stats2", [128, B, 6])
        mv2 = sb("mv2", [128, B, 2])
        var_eps2 = sb("var_eps2", [128, B])
        rstd2 = sb("rstd2", [128, B])
        row_max = sb("row_max", [128, B, H])
        max_rest = sb("max_rest", [128, B, H])
        neg_max = sb("neg_max", [128, B, 128], BF16)
        neg_maxT = sb("neg_maxT", [128, B, T], BF16)
        rden = sb("rden", [128, H])
        logits = sb("logits", [128, B, E_RT])
        pair_gt = sb("pair_gt", [128, B, E_RT, E_RT])
        pair_ge = sb("pair_ge", [128, B, E_RT, E_RT])
        rank = sb("rank", [128, B, E_RT])
        chosen = sb("chosen", [128, B, E_RT])
        top = sb("top", [128, B])
        shifted = sb("shifted", [128, B, E_RT])
        expo = sb("expo", [128, B, E_RT])
        gsum = sb("gsum", [128, B])
        grec = sb("grec", [128, B])
        gates = sb("gates", [128, B, E_RT])
        ident = sb("ident", [128, 128])
        ident_b = sb("ident_b", [128, 128], BF16)
        before = sb("before", [128, E_RT, E_RT])
        minus_half = sb("minus_half", [128, B])
        bo_rep = sb("bo_rep", [128, D])
        bv_rep = sb("bv_rep", [128, D])
        rb_rep = sb("rb_rep", [128, E_RT])
        bq_col = sb("bq_col", [128, C])
        bq_quarter = sb("bq_quarter", [128, C])
        bk_col = sb("bk_col", [128, C])

        misc = [pb("misc0"), pb("misc1")]
        s_bank = pb("s_bank")
        st_bank = [pb("st_bank0"), pb("st_bank1")]
        h1_bank = pb("h1_bank")
        h3_bank = pb("h3_bank")
        y_bank = pb("y_bank")
        front_bank = [s_bank, s_bank, s_bank, st_bank[0], st_bank[1], s_bank, st_bank[0], st_bank[1], st_bank[0]]
        turn_bank = [misc[0], s_bank]

        parts_dram = nc.dram_tensor("parts_dram", [2, PARTS, C, 128, TG], BF16, kind="Internal").ap()
        nm_dram = nc.dram_tensor("nm_dram", [B, PARTS * H, T], BF16, kind="Internal").ap()

        consts_in = sem("consts_in")
        stage_in = sem("stage_in")
        stage_hi = sem("stage_hi")
        stage_lo = sem("stage_lo")
        const_ready = sem("const_ready")
        pool_const = sem("pool_const")
        ident_in_done = sem("ident_in_done")
        x_loaded = sem("x_loaded")
        c_loaded = sem("c_loaded")
        var_ready = sem("var_ready")
        rstd_ready = sem("rstd_ready")
        xn_ready = sem("xn_ready")
        res_ready = sem("res_ready")
        front_full = sem("front_full")
        front_hi = sem("front_hi")
        front_lo = sem("front_lo")
        proj_ready = sem("proj_ready")
        part1_ready = sem("part1_ready")
        rest_ready = sem("rest_ready")
        part2_ready = sem("part2_ready")
        part3_ready = sem("part3_ready")
        v_ready = sem("v_ready")
        parts_out = sem("parts_out")
        stack_in = sem("stack_in")
        s_full = sem("s_full")
        s_max = sem("s_max")
        nm_ready = sem("nm_ready")
        nmT_full = sem("nmT_full")
        nmT_ready = sem("nmT_ready")
        nm_out = sem("nm_out")
        nm_in = [sem(f"nm_in{b}") for b in range(B)]
        st_full = [sem(f"st_full{i}") for i in range(2)]
        exp_done = [sem(f"exp_done{i}") for i in range(2)]
        pv_done = [sem(f"pv_done{i}") for i in range(2)]
        outT_ready = sem("outT_ready")
        out_tok_full = sem("out_tok_full")
        cat_ready = sem("cat_ready")
        catT_full = sem("catT_full")
        catT_hi_done = sem("catT_hi_done")
        catT_lo_done = sem("catT_lo_done")
        wo_full = sem("wo_full")
        x2_ready = sem("x2_ready")
        var2_ready = sem("var2_ready")
        rstd2_ready = sem("rstd2_ready")
        xn2_ready = sem("xn2_ready")
        dve_ln = sem("dve_ln")
        dve_att = sem("dve_att")
        dve_ffn = sem("dve_ffn")
        xn2T_full = sem("xn2T_full")
        xn2T_hi_done = sem("xn2T_hi_done")
        xn2T_lo_done = sem("xn2T_lo_done")
        logits_full = sem("logits_full")
        logits_out = sem("logits_out")
        shifted_ready = sem("shifted_ready")
        expo_ready = sem("expo_ready")
        h1_full = sem("h1_full")
        h3_full = sem("h3_full")
        tanh_done = sem("tanh_done")
        u_done = sem("u_done")
        v_done = sem("v_done")
        hid_hi_done = sem("hid_hi_done")
        hid_lo_done = sem("hid_lo_done")
        y_full = sem("y_full")
        acc_done = sem("acc_done")
        gates_step = sem("gates_step")
        out_done = sem("out_done")

        DVE_LN = 9
        DVE_ATT = 6 * B
        DVE_FFN = 8
        Y_USES = 2 * NE
        CONST_DMAS = 6

        def wait_if(eng, g, semaphore, value):
            if not (isinstance(g, int) and g == 0):
                eng.wait_ge(semaphore, value)

        def y_of(s, b):
            return (misc[1] if s >= SPARE_Y and b >= 2 else y_bank)[:, (b % 2) * D:(b % 2 + 1) * D]

        def in_slot(g, s, first):
            return s - first if g is not None and 0 <= s - first < B else None

        def in_groups(eng, body):
            body(0, None, None)
            body(1, 0, None)
            with eng.Fori(1, G - 1) as g:
                body(g + 1, g, g - 1)
            body(None, G - 1, G - 2)
            body(None, None, G - 1)

        block = stack.enter_context(nc.Block())

        @block.sync
        def _(sp):
            def rep(ap_1d, n):
                return ap_1d.rearrange("(a n) -> a n", a=1).broadcast_to([128, n])

            def load_x(first):
                sp.dma_start(x_in[:], x[bass.ds(first, B)].rearrange("b p d -> p b d")).then_inc(x_loaded, 16)

            def load_c(first):
                sp.dma_start(c_in[:], ctx_in[bass.ds(first, B)].rearrange("b p d -> p b d")).then_inc(c_loaded, 16)

            def store(g, first):
                sp.wait_ge(acc_done, (g + 1) * (NE * B))
                sp.dma_start(out[bass.ds(first, B)].rearrange("b p d -> p b d"), acc).then_inc(out_done, 16)

            def load_stage(n):
                sp.wait_ge(stage_hi, n)
                sp.wait_ge(stage_lo, n)
                shared, routed, width = ((sw1, rw1, C * HID), (sw3, rw3, C * HID), (sw2, rw2, D))[n - 1]
                for src, lo, hi in ((shared, 0, E_SH), (routed, E_SH, NE)):
                    dst = stage[:, lo * width:hi * width]
                    if n < 3:
                        for c in range(C):
                            sp.dma_start(dst.rearrange("p (e c h) -> p e c h", c=C, h=HID)[:, :, c, :],
                                         src[:, c * 128:(c + 1) * 128, :].rearrange("e p h -> p e h")).then_inc(stage_in, 16)
                    else:
                        sp.dma_start(dst.rearrange("p (e d) -> p e d", d=D),
                                     src.rearrange("e h d -> h e d")).then_inc(stage_in, 16)

            load_x(0)
            sp.dma_start(ident[:], ident_in).then_inc(ident_in_done, 16)
            load_c(0)
            for cols, src in ((slice(WQ, WK), Wq.rearrange("(c p) n -> p c n", c=C)),
                              (slice(WO, RW), Wo.rearrange("(c p) n -> p c n", c=C)),
                              (slice(RW, ATT_W), rw.rearrange("(c p) n -> p c n", c=C))):
                sp.dma_start(stage[:, cols].rearrange("p (c n) -> p c n", c=C), src).then_inc(stage_in, 16)
            sp.dma_start(stage[:, WK:WV], Wk).then_inc(stage_in, 16)
            sp.dma_start(stage[:, WV:WO], Wv).then_inc(stage_in, 16)
            sp.dma_start(bq_col[:], bq.rearrange("(c p) -> p c", c=C), allow_slow_non_contiguous=True).then_inc(consts_in, 16)
            sp.dma_start(bk_col[:], bk.rearrange("(c p) -> p c", c=C), allow_slow_non_contiguous=True).then_inc(consts_in, 16)
            sp.dma_start(bo_rep[:], rep(bo, D)).then_inc(consts_in, 16)
            sp.dma_start(bv_rep[:], rep(bv, D)).then_inc(consts_in, 16)
            sp.dma_start(rb_rep[:], rep(rb, E_RT)).then_inc(consts_in, 16)
            sp.dma_start(before[:], before_in).then_inc(consts_in, 16)
            load_stage(1)

            def body(gl, ga, gf):
                if gl is not None:
                    load_from = gl * B if isinstance(gl, int) else sp.snap(gl * B)
                if gf is not None:
                    store_to = (gf - 1) * B if isinstance(gf, int) else sp.snap((gf - 1) * B)
                if gl is not None and not (isinstance(gl, int) and gl == 0):
                    sp.wait_ge(res_ready, gl)
                    load_x(load_from)
                    sp.wait_ge(front_full, (gl - 1) * FRONT + CT + 1)
                    load_c(load_from)
                if gf is not None and not (isinstance(gf, int) and gf == 0):
                    store(gf - 1, store_to)
                if isinstance(ga, int) and ga == 0:
                    load_stage(2)
                for s in range(NE):
                    b = in_slot(ga, s, NMT_SLOT)
                    if b is not None:
                        sp.wait_ge(nmT_ready, ga * B + b + 1)
                        sp.dma_start(nm_dram[b], neg_maxT[0:PARTS * H, b, :]).then_inc(nm_out, 16)
                        sp.wait_ge(nm_out, (ga * B + b + 1) * 16)
                        sp.dma_start(q_stack[KD:KM, :, b * T:(b + 1) * T],
                                     nm_dram[b].rearrange("(s h) t -> s h t", s=PARTS)).then_inc(nm_in[b], 16)
                if isinstance(ga, int) and ga == 0:
                    load_stage(3)
                if gl is not None:
                    for side in range(2):
                        sp.wait_ge(part3_ready, gl * 4 + 2 * side + 2)
                        sp.dma_start(parts_dram[side].rearrange("s c p t -> p (s c) t"),
                                     parts[:, side].rearrange("p s c t -> p (s c) t")).then_inc(parts_out, 16)
                        sp.wait_ge(parts_out, gl * 32 + 16 * side + 16)
                        for j, s in enumerate((K_PART, Q_PART)[side]):
                            dst = (k_stack, q_stack)[side][j * DK:(j + 1) * DK, :, :]
                            sp.dma_start(dst, parts_dram[side, s].rearrange("c (h d) t -> d (c h) t", d=DK)).then_inc(stack_in, 16)

            body(0, None, None)
            body(1, 0, None)
            body(2, 1, 0)
            with sp.Fori(2, G - 1) as g:
                body(g + 1, g, g - 1)
            body(None, G - 1, G - 2)
            body(None, None, G - 1)
            store(G - 1, (G - 1) * B)
            sp.wait_ge(out_done, G * 16)

        @block.gpsimd
        def _(pool):
            pool.memset(minus_half[:], -0.5).then_inc(pool_const, 1)
            pool.wait_ge(pool_const, 1)
            pool.memset(v_aug[:, :, :, DK:VW], 1.0).then_inc(pool_const, 1)
            pool.wait_ge(pool_const, 2)
            pool.memset(neg_max[:], 0.0).then_inc(pool_const, 1)
            pool.wait_ge(pool_const, 3)
            pool.memset(k_stack[KD:128, :, :], 1.0).then_inc(pool_const, 1)
            pool.wait_ge(pool_const, 4)

            def body(gl, ga, gf):
                for s in range(NE):
                    if gl is not None and s == 4:
                        wait_if(pool, gl, front_full, gl * FRONT)
                        pool.wait_ge(dve_ln, (gl + 1) * DVE_LN)
                        pool.wait_ge(var_ready, gl + 1)
                        pool.tensor_tensor(rstd[:], var_eps[:], minus_half[:], ALU.pow).then_inc(rstd_ready, 1)
                        pool.wait_ge(pool_const, 4)
                        pool.wait_ge(rstd_ready, gl + 1)
                        for b in range(B):
                            pool.tensor_scalar(xn[:, b, :], x_in[:, b, :], mean[:, b:b + 1], rstd[:, b:b + 1],
                                               ALU.subtract, ALU.mult).then_inc(xn_ready, 1)
                    for q in range(NQ):
                        if q == 1 and gf is not None:
                            pool.wait_ge(hid_hi_done, gf * NE + s + 1)
                            pool.tensor_tensor(hid_lo[s % 2][:], hidden[s % 2], hid_hi[s % 2][:].bitcast(F32),
                                               ALU.subtract).then_inc(hid_lo_done, 1)
                        if gl is not None and (s, q) in OTHER_PARTS:
                            n = OTHER_PARTS[s, q]
                            side, m = divmod(n, 2)
                            pool.wait_ge(part2_ready, gl * 4 + n + 1)
                            wait_if(pool, gl, parts_out, gl * 32)
                            pool.tensor_tensor(parts[:, side, 2, m, :], proj[:, n % 2, :], parts[:, side, 1, m, :],
                                               ALU.subtract).then_inc(part3_ready, 1)
                    b = in_slot(ga, s, WO_SLOT)
                    if b is not None:
                        if b == 0:
                            wait_if(pool, ga, xn2T_full, ga * C)
                        pool.wait_ge(var2_ready, ga * B + b + 1)
                        pool.tensor_tensor(rstd2[:, b:b + 1], var_eps2[:, b:b + 1], minus_half[:, 0:1],
                                           ALU.pow).then_inc(rstd2_ready, 1)
                        pool.wait_ge(pool_const, 4)
                        pool.wait_ge(rstd2_ready, ga * B + b + 1)
                        pool.tensor_scalar(xn2[:, b, :], x2[:, b, :], mv2[:, b, 0:1], rstd2[:, b:b + 1],
                                           ALU.subtract, ALU.mult).then_inc(xn2_ready, 1)
                    if gl is not None and s == 7:
                        if isinstance(gl, int) and gl == 0:
                            pool.wait_ge(consts_in, CONST_DMAS * 16)
                        if ga is not None:
                            pool.wait_ge(x2_ready, (ga + 1) * B)
                        pool.tensor_tensor(x_res[:], x_in[:], bo_rep[:].unsqueeze(1).broadcast_to([128, B, D]),
                                           ALU.add).then_inc(res_ready, 1)
            in_groups(pool, body)

        @block.scalar
        def _(act):
            def split_stage(n):
                act.wait_ge(stage_in, STAGE_COUNT[n])
                lo, hi = STAGE_COLS[n]
                act.activation(w_hi[:, lo:hi], stage[:, 0:hi - lo], ACT.Copy).then_inc(stage_hi, 1)

            split_stage(0)

            def body(gl, ga, gf):
                def exponentials(b, q):
                    k, use = q % 2, b * (NQ // 2) + q // 2
                    act.wait_ge(st_full[k], ga * (B * NQ // 2) + use + 1)
                    if use:
                        act.wait_ge(pv_done[k], ga * (B * NQ // 2) + use)
                    act.activation(prob[k][:], st_bank[k][:], ACT.Exp).then_inc(exp_done[k], 1)

                for s in range(NE):
                    bn, bt, bw = (in_slot(ga, s, first) for first in (NMT_SLOT, ST_SLOT, WO_SLOT))
                    if gf is not None:
                        act.wait_ge(h1_full, gf * NE + s + 1)
                        if s:
                            act.wait_ge(v_done, gf * NE + s)
                        act.activation(gate_act, h1_bank[:], ACT.Tanh, scale=0.5).then_inc(tanh_done, 1)
                        if s == 0:
                            act.wait_ge(shifted_ready, gf + 1)
                            act.activation(expo[:], shifted[:], ACT.Exp).then_inc(expo_ready, 1)
                    if bn is not None:
                        act.wait_ge(nmT_full, ga * B + bn + 1)
                        act.activation(neg_maxT[0:PARTS * H, bn, :], misc[1][0:PARTS * H, 0:T // 2].bitcast(BF16),
                                       ACT.Copy).then_inc(nmT_ready, 1)
                    if bt is not None:
                        exponentials(bt, 0)
                    if bw is not None:
                        act.wait_ge(catT_full, ga * B + bw + 1)
                        act.activation(catT_hi[:], misc[1][:, 0:C * T].rearrange("p (c t) -> p c t", c=C),
                                       ACT.Copy).then_inc(catT_hi_done, 1)
                    if gf is not None:
                        act.wait_ge(v_done, gf * NE + s + 1)
                        act.activation(hid_hi[s % 2][:], hidden[s % 2], ACT.Copy).then_inc(hid_hi_done, 1)
                    for q in range(NQ):
                        if q and bt is not None:
                            exponentials(bt, q)
                        if gl is not None:
                            front_piece(gl, s, q)
                    if bt is not None:
                        act.wait_ge(pv_done[1], (ga * B + bt + 1) * (NQ // 2))
                        act.activation(outT[:], misc[0][:], ACT.Copy).then_inc(outT_ready, 1)
                    if isinstance(gl, int) and gl == 0 and s == 8:
                        split_stage(1)
                    if isinstance(ga, int) and ga == 0 and s in (3, 8):
                        split_stage(2 if s == 3 else 3)
                if ga is not None:
                    for c in range(C):
                        act.wait_ge(xn2T_full, ga * C + c + 1)
                        if gf is not None and c == 0:
                            act.wait_ge(h3_full, (gf + 1) * NE)
                        act.activation(xn2T_hi[:, c, :], turn_bank[c][:], ACT.Copy).then_inc(xn2T_hi_done, 1)

            def front_piece(gl, s, q):
                if (s, q) in SPLIT_T:
                    n = SPLIT_T[s, q]
                    dst = (cT_hi[:], xnT_hi[:, 0, :], xnT_hi[:, 1, :])[n]
                    act.wait_ge(front_full, gl * FRONT + CT + n + 1)
                    act.activation(dst, front_bank[CT + n][:], ACT.Copy).then_inc(front_hi, 1)
                if (s, q) in OTHER_PARTS:
                    n = OTHER_PARTS[s, q]
                    side, m = divmod(n, 2)
                    act.wait_ge(rest_ready, gl * 4 + n + 1)
                    act.activation(parts[:, side, 1, m, :], proj[:, n % 2, :], ACT.Copy).then_inc(part2_ready, 1)
                if (s, q) in FIRST_PART:
                    n = FIRST_PART[s, q]
                    side, m = divmod(n, 2)
                    if isinstance(gl, int) and gl == 0 and n == 0:
                        act.wait_ge(const_ready, 2)
                    act.wait_ge(front_full, gl * FRONT + K0 + n + 1)
                    if n >= 2:
                        act.wait_ge(part3_ready, gl * 4 + n - 1)
                    else:
                        wait_if(act, gl, part3_ready, gl * 4)
                    bias = (bk_col, bq_quarter)[side][:, m:m + 1]
                    act.activation(proj[:, n % 2, :], front_bank[K0 + n][:], ACT.Identity, bias=bias,
                                   scale=(1.0, DK ** -0.5)[side]).then_inc(proj_ready, 1)
                    wait_if(act, gl, parts_out, gl * 32)
                    act.wait_ge(proj_ready, gl * 4 + n + 1)
                    act.activation(parts[:, side, 0, m, :], proj[:, n % 2, :], ACT.Copy).then_inc(part1_ready, 1)

            in_groups(act, body)

        @block.vector
        def _(dve):
            dve.wait_ge(ident_in_done, 16)
            dve.tensor_copy(ident_b[:], ident[:]).then_inc(const_ready, 1)

            def split_stage(n):
                dve.wait_ge(stage_hi, n + 1)
                lo, hi = STAGE_COLS[n]
                dve.tensor_tensor(w_lo[:, lo:hi], stage[:, 0:hi - lo], w_hi[:, lo:hi].bitcast(F32),
                                  ALU.subtract).then_inc(stage_lo, 1)

            def accumulate(gf, s, b):
                dve.wait_ge(y_full, gf * Y_USES + 2 * s + b // 2 + 1)
                y = y_of(s, b)
                if s == 0:
                    if b == 0:
                        wait_if(dve, gf, out_done, gf * 16)
                        dve.wait_ge(x2_ready, (gf + 1) * B)
                    ins = dve.tensor_tensor(acc[:, b, :], y, x2[:, b, :], ALU.add)
                elif s < E_SH:
                    dve.wait_ge(acc_done, (gf * NE + s - 1) * B + b + 1)
                    ins = dve.tensor_tensor(acc[:, b, :], y, acc[:, b, :], ALU.add)
                else:
                    if s == E_SH and b == 0:
                        dve.wait_ge(gates_step, gf * 2 + 2)
                    dve.wait_ge(acc_done, (gf * NE + s - 1) * B + b + 1)
                    ins = dve.scalar_tensor_tensor(out=acc[:, b, :], in0=y, scalar=gates[:, b, s - E_SH:s - E_SH + 1],
                                                   in1=acc[:, b, :], op0=ALU.mult, op1=ALU.add)
                ins.then_inc(acc_done, 1)

            def body(gl, ga, gf):
                steps = {"ln": 0, "att": 0, "ffn": 0}

                def ln_step(ins, wait=True):
                    steps["ln"] += 1
                    ins.then_inc(dve_ln, 1)
                    if wait:
                        dve.wait_ge(dve_ln, gl * DVE_LN + steps["ln"])

                def att_step(ins):
                    steps["att"] += 1
                    ins.then_inc(dve_att, 1)
                    dve.wait_ge(dve_att, ga * DVE_ATT + steps["att"])

                def ffn_step(ins):
                    steps["ffn"] += 1
                    ins.then_inc(dve_ffn, 1)
                    dve.wait_ge(dve_ffn, gf * DVE_FFN + steps["ffn"])

                def row_maximum(b, q):
                    dve.wait_ge(s_full, (ga * B + b) * NQ + q + 1)
                    dve.tensor_reduce(row_max[:, b, 4 * q:4 * q + 4], s_bank[:].rearrange("p (h t) -> p h t", h=4),
                                      AX.X, ALU.max).then_inc(s_max, 1)

                def front_piece(s, q):
                    if (s, q) in SPLIT_T:
                        n = SPLIT_T[s, q]
                        hi = (cT_hi[:], xnT_hi[:, 0, :], xnT_hi[:, 1, :])[n]
                        lo = (cT_lo[:], xnT_lo[:, 0, :], xnT_lo[:, 1, :])[n]
                        dve.wait_ge(front_hi, gl * 3 + n + 1)
                        dve.tensor_tensor(lo, front_bank[CT + n][:], hi.bitcast(F32), ALU.subtract).then_inc(front_lo, 1)
                    if (s, q) in FIRST_PART:
                        n = FIRST_PART[s, q]
                        side, m = divmod(n, 2)
                        dve.wait_ge(part1_ready, gl * 4 + n + 1)
                        dve.tensor_tensor(proj[:, n % 2, :], proj[:, n % 2, :], parts[:, side, 0, m, :],
                                          ALU.subtract).then_inc(rest_ready, 1)
                    if (s, q) in TAKE_V:
                        n = TAKE_V[s, q]
                        if isinstance(gl, int) and gl == 0 and n == 0:
                            dve.wait_ge(pool_const, 2)
                        dve.wait_ge(front_full, gl * FRONT + V01 + n + 1)
                        dve.tensor_tensor(v_aug[:, 2 * n:2 * n + 2, :, 0:DK],
                                          front_bank[V01 + n][:].rearrange("p (b h d) -> p b h d", h=H, d=DK),
                                          bv_rep[:].rearrange("p (h d) -> p h d", d=DK).unsqueeze(1).broadcast_to([128, 2, H, DK]),
                                          ALU.add).then_inc(v_ready, 1)

                if gf is not None:
                    dve.wait_ge(logits_full, gf + 1)
                    dve.tensor_tensor(logits[:], misc[0][:, 0:B * E_RT].rearrange("p (b e) -> p b e", b=B),
                                      rb_rep[:].unsqueeze(1).broadcast_to([128, B, E_RT]), ALU.add).then_inc(logits_out, 1)
                    dve.wait_ge(logits_out, gf + 1)
                    ffn_step(dve.tensor_reduce(top[:], logits[:], AX.X, ALU.max))
                    dve.tensor_tensor(shifted[:], logits[:], top[:].unsqueeze(2).broadcast_to([128, B, E_RT]),
                                      ALU.subtract).then_inc(shifted_ready, 1)

                def turn_low():
                    for c in range(C):
                        dve.wait_ge(xn2T_hi_done, ga * C + c + 1)
                        dve.tensor_tensor(xn2T_lo[:, c, :], turn_bank[c][:], xn2T_hi[:, c, :].bitcast(F32),
                                          ALU.subtract).then_inc(xn2T_lo_done, 1)

                def choose():
                    other = logits[:].unsqueeze(2).broadcast_to([128, B, E_RT, E_RT])
                    own = logits[:].unsqueeze(3).broadcast_to([128, B, E_RT, E_RT])
                    ffn_step(dve.tensor_tensor(pair_ge[:], other, own, ALU.is_ge))
                    ffn_step(dve.tensor_tensor(pair_ge[:], pair_ge[:], before[:].unsqueeze(1).broadcast_to(
                        [128, B, E_RT, E_RT]), ALU.mult))
                    ffn_step(dve.tensor_tensor(pair_gt[:], other, own, ALU.is_gt))
                    ffn_step(dve.tensor_tensor(pair_gt[:], pair_gt[:], pair_ge[:], ALU.max))
                    ffn_step(dve.tensor_reduce(rank[:], pair_gt[:], AX.X, ALU.add))
                    dve.wait_ge(expo_ready, gf + 1)
                    ffn_step(dve.scalar_tensor_tensor(out=chosen[:], in0=rank[:], scalar=1.5, in1=expo[:],
                                                      op0=ALU.is_lt, op1=ALU.mult))
                    ffn_step(dve.tensor_reduce(gsum[:], chosen[:], AX.X, ALU.add))
                    dve.reciprocal(grec[:], gsum[:]).then_inc(gates_step, 1)
                    dve.wait_ge(gates_step, gf * 2 + 1)
                    dve.tensor_tensor(gates[:], chosen[:], grec[:].unsqueeze(2).broadcast_to(
                        [128, B, E_RT]), ALU.mult).then_inc(gates_step, 1)

                for s in range(NE):
                    bs, bw = (in_slot(ga, s, first) for first in (S_SLOT, WO_SLOT))
                    if gf is not None:
                        dve.wait_ge(tanh_done, gf * NE + s + 1)
                        dve.scalar_tensor_tensor(out=gate_act, in0=gate_act, scalar=1.0, in1=h1_bank[:],
                                                 op0=ALU.add, op1=ALU.mult).then_inc(u_done, 1)
                    if bw is not None:
                        tok = misc[0][:].rearrange("p (h d) -> p h d", h=H)
                        dve.wait_ge(out_tok_full, ga * B + bw + 1)
                        att_step(dve.reciprocal(rden[:], tok[:, :, DK]))
                        dve.tensor_tensor(cat[:].rearrange("p (h d) -> p h d", h=H), tok[:, :, 0:DK],
                                          rden[:].unsqueeze(2).broadcast_to([128, H, DK]), ALU.mult).then_inc(cat_ready, 1)
                    if bs is not None:
                        row_maximum(bs, 0)
                    if gf is not None:
                        dve.wait_ge(u_done, gf * NE + s + 1)
                        dve.wait_ge(h3_full, gf * NE + s + 1)
                        if s >= 2:
                            dve.wait_ge(hid_lo_done, gf * NE + s - 1)
                        dve.scalar_tensor_tensor(out=hidden[s % 2], in0=gate_act, scalar=0.5, in1=h3_bank[:],
                                                 op0=ALU.mult, op1=ALU.mult).then_inc(v_done, 1)
                    if bw is not None:
                        dve.wait_ge(catT_hi_done, ga * B + bw + 1)
                        dve.tensor_tensor(catT_lo[:], misc[1][:, 0:C * T].rearrange("p (c t) -> p c t", c=C),
                                          catT_hi[:].bitcast(F32), ALU.subtract).then_inc(catT_lo_done, 1)
                    for q in range(NQ):
                        if gf is not None and s and q == 0:
                            accumulate(gf, s - 1, 0)
                            accumulate(gf, s - 1, 1)
                        if q == 3 and bw is not None:
                            dve.wait_ge(dve_att, ga * DVE_ATT + steps["att"])
                        if gf is not None and s and q == 3:
                            if s == NE - 1 and ga is not None:
                                turn_low()
                            accumulate(gf, s - 1, 2)
                            accumulate(gf, s - 1, 3)
                        if q == 1 and bw is not None:
                            dve.wait_ge(wo_full, ga * B + bw + 1)
                            dve.wait_ge(res_ready, ga + 1)
                            if gf is not None and bw == 0:
                                dve.wait_ge(acc_done, gf * (NE * B) + B)
                            dve.tensor_tensor(x2[:, bw, :], misc[1][:, 0:D], x_res[:, bw, :], ALU.add).then_inc(x2_ready, 1)
                        if q and bs is not None:
                            row_maximum(bs, q)
                        if q == 1 and bw is not None:
                            dve.wait_ge(x2_ready, ga * B + bw + 1)
                            dve.bn_stats(stats2[:, bw, :], x2[:, bw, :]).then_inc(dve_att, 1)
                            steps["att"] += 1
                        if q == 3 and bw is not None:
                            dve.bn_aggr(mv2[:, bw, :], stats2[:, bw, :]).then_inc(dve_att, 1)
                            steps["att"] += 1
                            dve.wait_ge(dve_att, ga * DVE_ATT + steps["att"])
                            dve.tensor_scalar(var_eps2[:, bw:bw + 1], mv2[:, bw, 1:2], EPS, None,
                                              ALU.add).then_inc(var2_ready, 1)
                        if gl is not None:
                            front_piece(s, q)
                    if bs is not None:
                        nm = [neg_max[:, bs, p * H:(p + 1) * H] for p in range(PARTS)]
                        if isinstance(ga, int) and ga == 0 and bs == 0:
                            dve.wait_ge(pool_const, 3)
                        dve.wait_ge(s_max, (ga * B + bs + 1) * NQ)
                        wait_if(dve, ga, nmT_full, ga * B)
                        att_step(dve.tensor_scalar(nm[0], row_max[:, bs, :], -1.0, None, ALU.mult))
                        att_step(dve.scalar_tensor_tensor(out=max_rest[:, bs, :], in0=row_max[:, bs, :], scalar=-1.0,
                                                          in1=nm[0], op0=ALU.mult, op1=ALU.subtract))
                        att_step(dve.tensor_copy(nm[1], max_rest[:, bs, :]))
                        dve.tensor_tensor(nm[2], max_rest[:, bs, :], nm[1], ALU.subtract).then_inc(nm_ready, 1)
                    if gf is not None and s == 0:
                        choose()
                    if gl is not None and s < B:
                        if s == 0:
                            dve.wait_ge(x_loaded, (gl + 1) * 16)
                            wait_if(dve, gl, xn_ready, gl * B)
                        ln_step(dve.bn_stats(stats[:, s, :], x_in[:, s, :]), wait=False)
                    if gl is not None and s == B - 1:
                        even, odd = stats[:, :, 0:3], stats[:, :, 3:6]
                        dve.wait_ge(dve_ln, gl * DVE_LN + steps["ln"])
                        ln_step(dve.tensor_tensor(mean_parts[:, 0, :], even[:, :, 1], odd[:, :, 1], ALU.add), wait=False)
                        ln_step(dve.tensor_tensor(mean_parts[:, 1, :], even[:, :, 1], odd[:, :, 1], ALU.subtract), wait=False)
                        ln_step(dve.scalar_tensor_tensor(out=mean_parts[:, 2, :], in0=even[:, :, 2], scalar=D * EPS,
                                                         in1=odd[:, :, 2], op0=ALU.add, op1=ALU.add))
                        ln_step(dve.scalar_tensor_tensor(out=mean_parts[:, 1, :], in0=mean_parts[:, 1, :], scalar=0.25,
                                                         in1=mean_parts[:, 1, :], op0=ALU.mult, op1=ALU.mult))
                        dve.scalar_tensor_tensor(out=var_eps[:], in0=mean_parts[:, 2, :], scalar=1.0 / D,
                                                 in1=mean_parts[:, 1, :], op0=ALU.mult, op1=ALU.add).then_inc(var_ready, 1)
                        ln_step(dve.tensor_scalar(mean[:], mean_parts[:, 0, :], 0.5, None, ALU.mult))
                    if isinstance(gl, int) and gl == 0 and s == B:
                        split_stage(0)
                        dve.wait_ge(consts_in, CONST_DMAS * 16)
                        dve.tensor_scalar(bq_quarter[:], bq_col[:], DK ** -0.5, None, ALU.mult).then_inc(const_ready, 1)
                    if isinstance(gl, int) and gl == 0 and s == 8:
                        split_stage(1)
                    if isinstance(ga, int) and ga == 0 and s in (3, 8):
                        split_stage(2 if s == 3 else 3)
                if ga is not None and gf is None:
                    turn_low()
                if gf is not None:
                    for q in range(B):
                        accumulate(gf, NE - 1, q)
                assert gl is None or steps["ln"] == DVE_LN, steps
                assert ga is None or steps["att"] == DVE_ATT, steps
                assert gf is None or steps["ffn"] == DVE_FFN, steps

            in_groups(dve, body)

        @block.tensor
        def _(pe):
            def three(out_ap, terms):
                n = len(terms)
                for i, (lh, ll, rh, rl) in enumerate(terms):
                    pe.matmul(out_ap, lh, rh, start=(i == 0), stop=False)
                    pe.matmul(out_ap, ll, rh, start=False, stop=False)
                    ins = pe.matmul(out_ap, lh, rl, start=False, stop=(i == n - 1))
                return ins

            def weights(start, size):
                return w_hi[:, start:start + size], w_lo[:, start:start + size]

            pe.wait_ge(ident_in_done, 16)

            def front(gl, ga, use):
                bank = front_bank[use]
                if use == CT:
                    pe.wait_ge(c_loaded, (gl + 1) * 16)
                    if ga is not None:
                        pe.wait_ge(s_max, (ga + 1) * (B * NQ))
                    for b in range(B):
                        ins = pe.transpose(bank[:, b * T:(b + 1) * T], c_in[:, b, :], ident[:])
                elif use in (XT0, XT1):
                    m = use - XT0
                    pe.wait_ge(front_lo, gl * 3 + 1 + m)
                    if use == XT0:
                        pe.wait_ge(xn_ready, (gl + 1) * B)
                    for b in range(B):
                        ins = pe.transpose(bank[:, b * T:(b + 1) * T], xn[:, b, m * 128:(m + 1) * 128], ident[:])
                elif use in (K0, K1):
                    m = use - K0
                    if isinstance(gl, int) and gl == 0 and m == 0:
                        pe.wait_ge(stage_lo, 1)
                    if ga is not None:
                        pe.wait_ge(exp_done[m], (ga + 1) * (B * NQ // 2))
                    ins = three(bank[:], [(*weights(WK + m * 128, 128), cT_hi[:], cT_lo[:])])
                elif use in (Q0, Q1):
                    m = use - Q0
                    if m == 0:
                        pe.wait_ge(front_lo, gl * 3 + 3)
                    else:
                        pe.wait_ge(proj_ready, gl * 4 + 1)
                    ins = three(bank[:], [(*weights(WQ + c * D + m * 128, 128), xnT_hi[:, c, :], xnT_lo[:, c, :])
                                          for c in range(C)])
                else:
                    n = use - V01
                    pe.wait_ge(proj_ready, gl * 4 + (2, 4)[n])
                    for b in (2 * n, 2 * n + 1):
                        tok = slice(b * T, (b + 1) * T)
                        ins = three(bank[:, (b % 2) * D:(b % 2 + 1) * D],
                                    [(cT_hi[:, tok], cT_lo[:, tok], *weights(WV, D))])
                ins.then_inc(front_full, 1)

            def body(gl, ga, gf):
                def up(which, s):
                    bank, start = ((h1_bank, W1), (h3_bank, W3))[which]
                    if s == 0 and which == 0:
                        pe.wait_ge(stage_lo, 4)
                    if s:
                        pe.wait_ge((u_done, v_done)[which], gf * NE + s)
                    three(bank[:], [(*weights(start + (s * C + c) * HID, HID), xn2T_hi[:, c, :], xn2T_lo[:, c, :])
                                    for c in range(C)]).then_inc((h1_full, h3_full)[which], 1)

                def down(s, half):
                    k = s % 2
                    if half == 0:
                        pe.wait_ge(hid_lo_done, gf * NE + s + 1)
                    if s == SPARE_Y and half == 1:
                        if ga is not None:
                            pe.wait_ge(x2_ready, (ga + 1) * B)
                    elif s > SPARE_Y:
                        pe.wait_ge(acc_done, gf * (NE * B) + (s - 1) * B + 2 * half + 2)
                    elif s or half:
                        pe.wait_ge(acc_done, gf * (NE * B) + s * B + 2 * half)
                    else:
                        wait_if(pe, gf, acc_done, gf * (NE * B))
                    for b in (2 * half, 2 * half + 1):
                        tok = slice(b * T, (b + 1) * T)
                        ins = three(y_of(s, b),
                                    [(hid_hi[k][:, tok], hid_lo[k][:, tok], *weights(W2 + s * D, D))])
                    ins.then_inc(y_full, 1)

                def scores(b, q):
                    if b == 0 and q == 0:
                        pe.wait_ge(stack_in, (ga + 1) * (12 * 16))
                    else:
                        pe.wait_ge(s_max, (ga * B + b) * NQ + q)
                    tok = slice(b * T, (b + 1) * T)
                    for j in range(4):
                        ins = pe.matmul(s_bank[:, j * T:(j + 1) * T], q_stack[0:KD, 4 * q + j, tok],
                                        k_stack[0:KD, 4 * q + j, tok], start=True, stop=True)
                    ins.then_inc(s_full, 1)

                def scores_t(b, q):
                    k, use = q % 2, b * (NQ // 2) + q // 2
                    if q == 0:
                        if isinstance(ga, int) and ga == 0 and b == 0:
                            pe.wait_ge(pool_const, 4)
                        pe.wait_ge(nm_in[b], (ga + 1) * 16)
                    if use:
                        pe.wait_ge(exp_done[k], ga * (B * NQ // 2) + use)
                    else:
                        pe.wait_ge(v_ready, (ga + 1) * 2)
                    tok = slice(b * T, (b + 1) * T)
                    for j in range(4):
                        ins = pe.matmul(st_bank[k][:, j * T:(j + 1) * T], k_stack[0:KM, 4 * q + j, tok],
                                        q_stack[0:KM, 4 * q + j, tok], start=True, stop=True)
                    ins.then_inc(st_full[k], 1)

                def values(b, q):
                    k, use = q % 2, b * (NQ // 2) + q // 2
                    pe.wait_ge(exp_done[k], ga * (B * NQ // 2) + use + 1)
                    if q == 0 and b == 0:
                        if gf is not None:
                            pe.wait_ge(logits_out, gf + 1)
                    elif q == 0:
                        pe.wait_ge(cat_ready, ga * B + b)
                    for j in range(4):
                        ins = pe.matmul(misc[0][j * VW:(j + 1) * VW, q * T:(q + 1) * T], v_aug[:, b, 4 * q + j, :],
                                        prob[k][:, j * T:(j + 1) * T], start=True, stop=True)
                    ins.then_inc(pv_done[k], 1)

                for s in range(NE):
                    bs, bn, bt, bw = (in_slot(ga, s, first) for first in (S_SLOT, NMT_SLOT, ST_SLOT, WO_SLOT))
                    if gf is not None:
                        up(0, s)
                    if bn is not None:
                        pe.wait_ge(nm_ready, ga * B + bn + 1)
                        if bn == 0:
                            if gf is not None:
                                wait_if(pe, gf, acc_done, gf * (NE * B))
                        elif bw:
                            pe.wait_ge(x2_ready, ga * B + bw)
                        else:
                            pe.wait_ge(nmT_ready, ga * B + bn)
                        if isinstance(ga, int) and ga == 0 and bn == 0:
                            pe.wait_ge(const_ready, 1)
                        pe.transpose(misc[1][:, 0:T // 2].bitcast(BF16), neg_max[:, bn, :],
                                     ident_b[:]).then_inc(nmT_full, 1)
                    if bw is not None:
                        pe.wait_ge(outT_ready, ga * B + bw + 1)
                        for q in range(NQ):
                            ins = pe.transpose(misc[0][:, q * T:(q + 1) * T], outT[:, q * T:(q + 1) * T], ident[:])
                        ins.then_inc(out_tok_full, 1)
                    if bs is not None:
                        scores(bs, 0)
                    if gf is not None:
                        up(1, s)
                    if bt is not None:
                        scores_t(bt, 0)
                    if bw is not None:
                        pe.wait_ge(cat_ready, ga * B + bw + 1)
                        if bn is not None:
                            pe.wait_ge(nmT_ready, ga * B + bn + 1)
                        elif bw:
                            pe.wait_ge(x2_ready, ga * B + bw)
                        for c in range(C):
                            ins = pe.transpose(misc[1][:, c * T:(c + 1) * T], cat[:, c * 128:(c + 1) * 128], ident[:])
                        ins.then_inc(catT_full, 1)
                    for q in range(NQ):
                        if gf is not None and s and q in (0, 3):
                            down(s - 1, q // 3)
                        if q and bs is not None:
                            scores(bs, q)
                        if q and bt is not None:
                            scores_t(bt, q)
                            values(bt, q - 1)
                        if q == 1 and bw is not None:
                            pe.wait_ge(catT_lo_done, ga * B + bw + 1)
                            three(misc[1][:, 0:D], [(catT_hi[:, c, :], catT_lo[:, c, :], *weights(WO + c * D, D))
                                                    for c in range(C)]).then_inc(wo_full, 1)
                        if gl is not None and (s, q) in FRONT_PE:
                            front(gl, ga, FRONT_PE[s, q])
                        if ga is not None and (s, q) == TURN:
                            pe.wait_ge(xn2_ready, (ga + 1) * B)
                            if gl is not None:
                                pe.wait_ge(proj_ready, gl * 4 + 3)
                            else:
                                pe.wait_ge(s_max, (ga + 1) * (B * NQ))
                            for c in range(C):
                                for b in range(B):
                                    ins = pe.transpose(turn_bank[c][:, b * T:(b + 1) * T],
                                                       xn2[:, b, c * 128:(c + 1) * 128], ident[:])
                                ins.then_inc(xn2T_full, 1)
                    if bt is not None:
                        values(bt, NQ - 1)
                if gf is not None:
                    down(NE - 1, 0)
                    down(NE - 1, 1)
                if ga is not None:
                    pe.wait_ge(xn2T_lo_done, (ga + 1) * C)
                    for b in range(B):
                        tok = slice(b * T, (b + 1) * T)
                        ins = three(misc[0][:, b * E_RT:(b + 1) * E_RT],
                                    [(xn2T_hi[:, c, tok], xn2T_lo[:, c, tok], *weights(RW + c * E_RT, E_RT))
                                     for c in range(C)])
                    ins.then_inc(logits_full, 1)
            in_groups(pe, body)

_INS = ["x", "ctx_512", "L0_xattn_Wq", "L0_xattn_bq", "L0_xattn_Wk", "L0_xattn_bk", "L0_xattn_Wv", "L0_xattn_bv",
        "L0_xattn_Wo", "L0_xattn_bo", "L0_ffn_router_w", "L0_ffn_router_b", "L0_ffn_routed_w1", "L0_ffn_routed_w3",
        "L0_ffn_routed_w2", "L0_ffn_shared_w1", "L0_ffn_shared_w3", "L0_ffn_shared_w2"]


def kernel(**inputs):
    import numpy as np
    import concourse.bacc as bacc
    from concourse import mybir as mb
    from concourse.bass_utils import run_bass_kernel_spmd as run

    nc = bacc.Bacc("TRN2", target_bir_lowering=False, num_devices=1)
    arrays, args = {}, []
    given = [(name, np.ascontiguousarray(inputs[name])) for name in _INS]
    given.append(("identity", np.eye(128, dtype=np.float32)))
    lower = np.tri(E_RT, E_RT, -1, dtype=np.float32)
    given.append(("before", np.ascontiguousarray(np.broadcast_to(lower, (128, E_RT, E_RT)))))
    for name, a in given:
        arrays[f"in_{name}"] = a
        args.append(nc.dram_tensor(f"in_{name}", a.shape, mb.dt.from_np(a.dtype), kind="ExternalInput").ap())
    args.append(nc.dram_tensor("out_x", (NB, T, D), F32, kind="ExternalOutput").ap())
    build(nc, *args)
    r = run(nc, [arrays], core_ids=[0])
    return r.results[0]["out_x"]
```

```python
from contextlib import ExitStack

import concourse.bass as bass
from concourse import mybir

F32 = mybir.dt.float32
F32R = mybir.dt.float32r
BF16 = mybir.dt.bfloat16
ALU = mybir.AluOpType
ACT = mybir.ActivationFunctionType
AX = mybir.AxisListType

NB, T, D = 32, 128, 256
DC = 128
H, DK = 16, 16
E_SH, E_RT, HID = 2, 8, 128
NE = E_SH + E_RT
B = 4
G = NB // B
TG = B * T
C = D // 128
HC = 128 // DK
NQ = H // 4
EPS = 1e-5
PARTS = 3
Q_PART = [0, 1, 2, 0, 1, 0]
K_PART = [2, 1, 0, 1, 0, 0]
RUNS = [[(0, 3, 0), (3, 2, 0), (5, 1, 0)], [(0, 3, 0), (3, 2, 1), (5, 1, 2)]]
KD = len(Q_PART) * DK
KM = KD + PARTS
VW = 32

WQ = 0
WK = WQ + C * D
WV = WK + D
WO = WV + D
ATT_W = WO + C * D
RW = ATT_W
W1 = ATT_W
W3 = W1 + NE * C * HID
W2 = W3 + NE * C * HID
ALL_W = W2 + NE * D
FFN_W = NE * C * HID

STAGE_COLS = [(0, ATT_W), (W1, W3), (W3, W2), (W2, ALL_W)]
STAGE_COUNT = [5 * 16, 9 * 16, 13 * 16, 15 * 16]

FRONT = 9
XT0, XT1, CT, Q0, Q1, K0, K1, V01, V23 = range(FRONT)
FRONT_PE = {(4, 0): XT0, (4, 3): XT1, (5, 0): CT, (5, 3): Q0, (6, 0): Q1, (6, 1): K0, (6, 3): K1, (9, 0): V01}
SPLIT_T = {(4, 0): 0, (4, 3): 1, (5, 0): 2}
FIRST_PART = {(5, 3): 0, (6, 0): 1, (6, 1): 2, (7, -1): 3}
OTHER_PARTS = {(6, -1): 0, (6, 2): 1, (6, 3): 2, (7, 1): 3}
TAKE_V = {(9, 0): 0}
V23_SLOT = 1

WARM_START, WARM_STACKS = 20, 76
HI2, LO2, LD3, HI3, LO3 = 1, 1, 3, 4, 5
XN_SLOT = 3
TURN = 8
SPARE_Y = 6
S_SLOT, NMT_SLOT, ST_SLOT, WO_SLOT, XN2_SLOT = 0, 1, 2, 3, 4
LIGHT = (0, 1)
RES_SLOT = 4
CHOOSE = {(0, 1): 0, (0, 2): 1, (1, 1): 2, (1, 2): 3, (1, 3): 4, (2, 1): 5, (2, 2): 6}
ACC_FIRST = {2: 1, 3: 1, 6: 0}
STATS = {2: (0, 1, 2, 3)}


def build(nc, x, ctx_in, Wq, bq, Wk, bk, Wv, bv, Wo, bo, rw, rb, rw1, rw3, rw2, sw1, sw3, sw2,
          ident_in, before_in, out):
    with ExitStack() as stack:
        def sb(name, shape, dt=F32):
            return stack.enter_context(nc.sbuf_tensor(name, shape, dt))

        def pb(name, shape=(128, 512), dt=F32):
            return stack.enter_context(nc.psum_tensor(name, list(shape), dt))

        def sem(name):
            return stack.enter_context(nc.semaphore(name))

        w_hi = sb("w_hi", [128, ALL_W], F32R)
        w_lo = sb("w_lo", [128, ALL_W], F32R)
        router = sb("router", [128, C, 2 * E_RT], F32R)
        ffn_f32 = sb("ffn_f32", [128, FFN_W])
        acc = ffn_f32[:, 0:B * D].rearrange("p (b d) -> p b d", b=B)
        gate_act = ffn_f32[:, B * D:B * D + TG]
        hidden = [ffn_f32[:, B * D + (1 + i) * TG:B * D + (2 + i) * TG] for i in range(2)]
        stage = ffn_f32

        x_in = sb("x_in", [128, B, D])
        x_res = sb("x_res", [128, B, D])
        shared_buf = sb("shared_buf", [128, B, D])
        finished = xn = shared_buf
        proj = shared_buf[:].rearrange("p b d -> p (b d)").rearrange("p (n t) -> p n t", n=2)
        x2 = sb("x2", [128, B, D])
        xn2 = sb("xn2", [128, B, D])
        c_in = sb("c_in", [128, B, DC])
        xnT_hi = sb("xnT_hi", [128, C, TG], F32R)
        xnT_lo = sb("xnT_lo", [128, C, TG], F32R)
        cT_hi = sb("cT_hi", [128, TG], F32R)
        cT_lo = sb("cT_lo", [128, TG], F32R)
        xn2T_hi = sb("xn2T_hi", [128, C, TG], F32R)
        xn2T_lo = sb("xn2T_lo", [128, C, TG], F32R)
        parts = sb("parts", [128, 2, PARTS, C, TG], BF16)
        q_stack = sb("q_stack", [128, H, TG], BF16)
        k_stack = sb("k_stack", [128, H, TG], BF16)
        v_aug = sb("v_aug", [128, B, H, VW])
        outT = sb("outT", [128, NQ * T])
        prob = [sb(f"prob{i}", [128, 4 * T]) for i in range(2)]
        cat = sb("cat", [128, D])
        catT_hi = sb("catT_hi", [128, C, T], F32R)
        catT_lo = sb("catT_lo", [128, C, T], F32R)
        hid_hi = [sb(f"hid_hi{i}", [128, TG], F32R) for i in range(2)]
        hid_lo = [sb(f"hid_lo{i}", [128, TG], F32R) for i in range(2)]
        y_gated = sb("y_gated", [128, 2, 2, D])
        stats = sb("stats", [128, B, 6])
        mean_parts = sb("mean_parts", [128, 3, B])
        mean = sb("mean", [128, B])
        var_eps = sb("var_eps", [128, B])
        rstd = sb("rstd", [128, B])
        stats2 = sb("stats2", [128, B, 6])
        mv2 = sb("mv2", [128, B, 2])
        var_eps2 = sb("var_eps2", [128, B])
        rstd2 = sb("rstd2", [128, B])
        row_max = sb("row_max", [128, B, H])
        max_rest = sb("max_rest", [128, B, H])
        neg_max = sb("neg_max", [128, B, 128], BF16)
        neg_maxT = sb("neg_maxT", [128, B, T], BF16)
        rden = sb("rden", [128, H])
        logits = sb("logits", [128, B, E_RT])
        pair_gt = sb("pair_gt", [128, B, E_RT, E_RT])
        pair_eq = sb("pair_eq", [128, B, E_RT, E_RT])
        rank = sb("rank", [128, B, E_RT])
        chosen = sb("chosen", [128, B, E_RT])
        top = sb("top", [128, B])
        shifted = sb("shifted", [128, B, E_RT])
        expo = sb("expo", [128, B, E_RT])
        gsum = sb("gsum", [128, B])
        grec = sb("grec", [128, B])
        gates = sb("gates", [128, B, E_RT])
        ident = sb("ident", [128, 128])
        ident_b = sb("ident_b", [128, 128], BF16)
        before = sb("before", [128, E_RT, E_RT])
        minus_half = sb("minus_half", [128, B])
        bo_rep = sb("bo_rep", [128, D])
        bv_rep = sb("bv_rep", [128, D])
        rb_rep = sb("rb_rep", [128, E_RT])
        bq_col = sb("bq_col", [128, C])
        bq_quarter = sb("bq_quarter", [128, C])
        bk_col = sb("bk_col", [128, C])

        misc = [pb("misc0"), pb("misc1")]
        s_bank = pb("s_bank")
        st_bank = [pb("st_bank0"), pb("st_bank1")]
        h1_bank = pb("h1_bank")
        h3_bank = pb("h3_bank")
        y_bank = pb("y_bank")
        front_bank = [s_bank, s_bank, s_bank, s_bank, st_bank[0], st_bank[1], s_bank, st_bank[0], st_bank[1]]
        turn_bank = [misc[0], s_bank]

        def turned_in(g, n):
            return (s_bank, misc[0], misc[1])[n] if isinstance(g, int) and g == 0 else s_bank

        parts_dram = nc.dram_tensor("parts_dram", [2, C, HC, PARTS, DK, TG], BF16, kind="Internal").ap()

        consts_in = sem("consts_in")
        stage_in = sem("stage_in")
        stage_hi = sem("stage_hi")
        stage_lo = sem("stage_lo")
        router_hi = sem("router_hi")
        const_ready = sem("const_ready")
        pool_const = sem("pool_const")
        ident_in_done = sem("ident_in_done")
        x_loaded = sem("x_loaded")
        c_loaded = sem("c_loaded")
        var_ready = sem("var_ready")
        rstd_ready = sem("rstd_ready")
        xn01_ready = sem("xn01_ready")
        xn23_ready = sem("xn23_ready")
        res_ready = sem("res_ready")
        front_full = sem("front_full")
        front_hi = sem("front_hi")
        front_lo = sem("front_lo")
        proj_ready = sem("proj_ready")
        part1_ready = sem("part1_ready")
        rest_ready = sem("rest_ready")
        part2_ready = sem("part2_ready")
        part3_ready = sem("part3_ready")
        v_ready = sem("v_ready")
        parts_out = [sem(f"parts_out{m}") for m in range(C)]
        stack_in = [sem(f"stack_in{m}") for m in range(C)]
        s_full = sem("s_full")
        s_max = sem("s_max")
        nm_ready = sem("nm_ready")
        nmT_full = sem("nmT_full")
        nmT_ready = sem("nmT_ready")
        nm_in = [sem(f"nm_in{b}") for b in range(B)]
        st_full = [sem(f"st_full{i}") for i in range(2)]
        exp_done = [sem(f"exp_done{i}") for i in range(2)]
        pv_done = [sem(f"pv_done{i}") for i in range(2)]
        outT_ready = sem("outT_ready")
        out_tok_full = sem("out_tok_full")
        cat_ready = sem("cat_ready")
        catT_full = sem("catT_full")
        catT_hi_done = sem("catT_hi_done")
        catT_lo_done = sem("catT_lo_done")
        wo_full = sem("wo_full")
        x2_ready = sem("x2_ready")
        var2_ready = sem("var2_ready")
        rstd2_ready = sem("rstd2_ready")
        xn2_ready = sem("xn2_ready")
        dve_ln = sem("dve_ln")
        dve_att = sem("dve_att")
        dve_ffn = sem("dve_ffn")
        xn2T_full = sem("xn2T_full")
        xn2T_hi_done = sem("xn2T_hi_done")
        xn2T_lo_done = sem("xn2T_lo_done")
        logits_full = sem("logits_full")
        logits_out = sem("logits_out")
        shifted_ready = sem("shifted_ready")
        expo_ready = sem("expo_ready")
        h1_full = sem("h1_full")
        h3_full = sem("h3_full")
        tanh_done = sem("tanh_done")
        u_done = sem("u_done")
        v_done = sem("v_done")
        hid_hi_done = sem("hid_hi_done")
        hid_lo_done = sem("hid_lo_done")
        y_full = sem("y_full")
        y_taken = sem("y_taken")
        y01_taken = sem("y01_taken")
        acc01_done = sem("acc01_done")
        acc23_done = sem("acc23_done")
        pairs_ready = sem("pairs_ready")
        pair_before = sem("pair_before")
        gates_ready = sem("gates_ready")
        out_done = sem("out_done")

        DVE_LN = 9
        DVE_ATT = 6 * B
        DVE_FFN = 6
        CONST_DMAS = 6

        def wait_if(eng, g, semaphore, value):
            if not (isinstance(g, int) and g == 0):
                eng.wait_ge(semaphore, value)

        def score_bank(b, q):
            return st_bank[q // 2] if b < 2 and q % 2 else s_bank

        def y_of(s, b, alone=False):
            bank = y_bank if b < 2 or (0 < s < SPARE_Y and not alone) else misc[1] if s else misc[0]
            return bank[:, (b % 2) * D:(b % 2 + 1) * D]

        def wait_if_counted(eng, gf, s, semaphore, value):
            if not (isinstance(gf, int) and gf == 0 and s == 1):
                eng.wait_ge(semaphore, value)

        def in_slot(g, s, first):
            return s - first if g is not None and 0 <= s - first < B else None

        def in_groups(eng, body):
            body(0, None, None)
            body(1, 0, None)
            body(2, 1, 0)
            with eng.Fori(2, G - 1) as g:
                body(g + 1, g, g - 1)
            body(None, G - 1, G - 2)
            body(None, None, G - 1)

        def before_slot(gf, s):
            if gf is None or (isinstance(gf, int) and gf == 0 and s == 0):
                return None
            return (s - 1) % NE, gf * NE + s - 1

        def y01_count(gf, s):
            return gf * (2 * len(LIGHT)) + (0 if s else -2)

        block = stack.enter_context(nc.Block())

        @block.sync
        def _(sp):
            def rep(ap_1d, n):
                return ap_1d.rearrange("(a n) -> a n", a=1).broadcast_to([128, n])

            def load_x(first):
                sp.dma_start(x_in[:], x[bass.ds(first, B)].rearrange("b p d -> p b d")).then_inc(x_loaded, 16)

            def load_c(first):
                sp.dma_start(c_in[:], ctx_in[bass.ds(first, B)].rearrange("b p d -> p b d")).then_inc(c_loaded, 16)

            def store(g, first):
                sp.wait_ge(acc01_done, (g + 1) * (NE * 2))
                sp.wait_ge(acc23_done, (g + 1) * (NE * 2))
                sp.dma_start(out[bass.ds(first, B)].rearrange("b p d -> p b d"), finished[:]).then_inc(out_done, 16)

            def load_stage(n):
                sp.wait_ge(stage_hi, n)
                sp.wait_ge(stage_lo, n)
                shared, routed, width = ((sw1, rw1, C * HID), (sw3, rw3, C * HID), (sw2, rw2, D))[n - 1]
                for src, lo, hi in ((shared, 0, E_SH), (routed, E_SH, NE)):
                    dst = stage[:, lo * width:hi * width]
                    if n < 3:
                        for c in range(C):
                            sp.dma_start(dst.rearrange("p (e c h) -> p e c h", c=C, h=HID)[:, :, c, :],
                                         src[:, c * 128:(c + 1) * 128, :].rearrange("e p h -> p e h")).then_inc(stage_in, 16)
                    else:
                        sp.dma_start(dst.rearrange("p (e d) -> p e d", d=D),
                                     src.rearrange("e h d -> h e d")).then_inc(stage_in, 16)

            load_x(0)
            sp.dma_start(ident[:], ident_in).then_inc(ident_in_done, 16)
            load_c(0)
            for cols, src in ((slice(WQ, WK), Wq.rearrange("(c p) n -> p c n", c=C)),
                              (slice(WO, ATT_W), Wo.rearrange("(c p) n -> p c n", c=C)),
                              (slice(RW, RW + C * E_RT), rw.rearrange("(c p) n -> p c n", c=C))):
                sp.dma_start(stage[:, cols].rearrange("p (c n) -> p c n", c=C), src).then_inc(stage_in, 16)
            sp.dma_start(stage[:, WK:WV], Wk).then_inc(stage_in, 16)
            sp.dma_start(stage[:, WV:WO], Wv).then_inc(stage_in, 16)
            sp.dma_start(bq_col[:], bq.rearrange("(c p) -> p c", c=C), allow_slow_non_contiguous=True).then_inc(consts_in, 16)
            sp.dma_start(bk_col[:], bk.rearrange("(c p) -> p c", c=C), allow_slow_non_contiguous=True).then_inc(consts_in, 16)
            sp.dma_start(bo_rep[:], rep(bo, D)).then_inc(consts_in, 16)
            sp.dma_start(bv_rep[:], rep(bv, D)).then_inc(consts_in, 16)
            sp.dma_start(rb_rep[:], rep(rb, E_RT)).then_inc(consts_in, 16)
            sp.dma_start(before[:], before_in).then_inc(consts_in, 16)
            load_stage(1)

            def body(gl, ga, gf):
                if gl is not None:
                    load_from = gl * B if isinstance(gl, int) else sp.snap(gl * B)
                if gf is not None:
                    store_to = (gf - 1) * B if isinstance(gf, int) else sp.snap((gf - 1) * B)
                if gl is not None and not (isinstance(gl, int) and gl == 0):
                    sp.wait_ge(res_ready, gl * B)
                    load_x(load_from)
                    sp.wait_ge(front_full, (gl - 1) * FRONT + CT + 1)
                    load_c(load_from)
                if gf is not None and not (isinstance(gf, int) and gf == 0):
                    store(gf - 1, store_to)
                if isinstance(ga, int) and ga == 0:
                    load_stage(2)
                for s in range(NE):
                    if isinstance(ga, int) and ga == 0 and s == LD3:
                        load_stage(3)
                    b = in_slot(ga, s, NMT_SLOT)
                    if b is not None:
                        sp.wait_ge(nmT_ready, ga * B + b + 1)
                        for part in range(PARTS):
                            sp.dma_start(q_stack[KD + part:KD + part + 1, :, b * T:(b + 1) * T],
                                         neg_maxT[part * H:(part + 1) * H, b, :]).then_inc(nm_in[b], 16)
                if gl is not None:
                    for out_piece, in_piece in ((0, 0), (1, None), (2, 1), (3, 2), (None, 3)):
                        if out_piece is not None:
                            n, (side, m) = out_piece, divmod(out_piece, 2)
                            for part, ready in enumerate((part1_ready, part2_ready, part3_ready)):
                                sp.wait_ge(ready, gl * 4 + n + 1)
                                sp.dma_start(parts_dram[side, m, :, (part, PARTS - 1 - part)[side]],
                                             parts[:, side, part, m, :]).then_inc(parts_out[m], 16)
                        if in_piece is not None:
                            n, (side, m) = in_piece, divmod(in_piece, 2)
                            sp.wait_ge(parts_out[m], (gl * 2 + side + 1) * (PARTS * 16))
                            for block, count, first in RUNS[side]:
                                dst = (q_stack, k_stack)[side][block * DK:(block + count) * DK, m * HC:(m + 1) * HC, :]
                                sp.dma_start(dst, parts_dram[side, m, :, first:first + count].rearrange(
                                    "h s d t -> (s d) h t")).then_inc(stack_in[m], 16)

            in_groups(sp, body)
            store(G - 1, (G - 1) * B)
            sp.wait_ge(out_done, G * 16)

        @block.gpsimd
        def _(pool):
            pool.memset(minus_half[:], -0.5).then_inc(pool_const, 1)
            pool.wait_ge(pool_const, 1)
            pool.memset(v_aug[:, :, :, DK:VW], 1.0).then_inc(pool_const, 1)
            pool.wait_ge(pool_const, 2)
            pool.memset(neg_max[:], 0.0).then_inc(pool_const, 1)
            pool.wait_ge(pool_const, 3)

            def accumulate(gf, s):
                e, count = before_slot(gf, s)
                for b in range(B) if s in LIGHT else (2, 3):
                    done, n = (acc01_done, b) if b < 2 else (acc23_done, b - 2)
                    if b < 2:
                        pool.wait_ge(y01_taken, y01_count(gf, s) + n + 1)
                    else:
                        pool.wait_ge(y_taken, count * 2 + n + 1)
                    wait_if_counted(pool, gf, s, done, count * 2 + n)
                    y = y_gated[:, e % 2, n, :] if b >= 2 else prob[s][:, n * D:(n + 1) * D]
                    pool.tensor_tensor((finished if e == NE - 1 else acc)[:, b, :], y,
                                       (x2 if e == 0 else acc)[:, b, :], ALU.add).then_inc(done, 1)

            def body(gl, ga, gf):
                for s in range(NE):
                    if gl is not None and s == XN_SLOT:
                        wait_if(pool, gl, part3_ready, gl * 4)
                        if gf is not None:
                            wait_if(pool, gf, out_done, gf * 16)
                        pool.wait_ge(dve_ln, (gl + 1) * DVE_LN)
                        pool.wait_ge(var_ready, gl + 1)
                        pool.tensor_tensor(rstd[:], var_eps[:], minus_half[:], ALU.pow).then_inc(rstd_ready, 1)
                        pool.wait_ge(pool_const, 3)
                        pool.wait_ge(rstd_ready, gl + 1)
                        for b in () if isinstance(gl, int) and gl == 0 else (2, 3):
                            pool.tensor_scalar(xn[:, b, :], x_in[:, b, :], mean[:, b:b + 1], rstd[:, b:b + 1],
                                               ALU.subtract, ALU.mult).then_inc(xn23_ready, 1)
                    b = in_slot(ga, s, XN2_SLOT)
                    if b is not None:
                        pool.wait_ge(var2_ready, ga * B + b + 1)
                        pool.tensor_tensor(rstd2[:, b:b + 1], var_eps2[:, b:b + 1], minus_half[:, 0:1],
                                           ALU.pow).then_inc(rstd2_ready, 1)
                    for q in range(-1, NQ):
                        if q == 1 and gf is not None:
                            pool.wait_ge(hid_hi_done, gf * NE + s + 1)
                            pool.tensor_tensor(hid_lo[s % 2][:], hidden[s % 2], hid_hi[s % 2][:].bitcast(F32),
                                               ALU.subtract).then_inc(hid_lo_done, 1)
                        if gl is not None and (s, q) in OTHER_PARTS:
                            n = OTHER_PARTS[s, q]
                            side, m = divmod(n, 2)
                            pool.wait_ge(part2_ready, gl * 4 + n + 1)
                            wait_if(pool, gl, parts_out[m], gl * (2 * PARTS * 16))
                            pool.tensor_tensor(parts[:, side, 2, m, :], proj[:, n % 2, :], parts[:, side, 1, m, :],
                                               ALU.subtract).then_inc(part3_ready, 1)
                    if gf is not None and s == 0:
                        pool.wait_ge(pairs_ready, gf * 2 + 1)
                        pool.tensor_tensor(pair_eq[:], pair_eq[:], before[:].unsqueeze(1).broadcast_to(
                            [128, B, E_RT, E_RT]), ALU.mult).then_inc(pair_before, 1)
                        pool.wait_ge(pair_before, gf * 2 + 1)
                        pool.wait_ge(pairs_ready, gf * 2 + 2)
                        pool.tensor_tensor(pair_gt[:], pair_gt[:], pair_eq[:], ALU.add).then_inc(pair_before, 1)
                    if isinstance(gl, int) and gl == 0 and s == XN_SLOT:
                        pool.memset(k_stack[KD:128, :, :], 1.0).then_inc(pool_const, 1)
                        pool.wait_ge(pool_const, 4)
                    if before_slot(gf, s):
                        if s == 0 and ga is not None:
                            pool.wait_ge(part3_ready, (ga + 1) * 4)
                        accumulate(gf, s)
                    if isinstance(ga, int) and ga == 0 and s in (LO2, LO3):
                        n = 2 if s == LO2 else 3
                        pool.wait_ge(stage_hi, n + 1)
                        lo, hi = STAGE_COLS[n]
                        pool.tensor_tensor(w_lo[:, lo:hi], stage[:, 0:hi - lo], w_hi[:, lo:hi].bitcast(F32),
                                           ALU.subtract).then_inc(stage_lo, 1)
                    b = s - RES_SLOT
                    if gl is not None and 0 <= b < B:
                        if isinstance(gl, int) and gl == 0 and b == 0:
                            pool.wait_ge(consts_in, CONST_DMAS * 16)
                        if ga is not None:
                            pool.wait_ge(x2_ready, ga * B + b + 1)
                        pool.tensor_tensor(x_res[:, b, :], x_in[:, b, :], bo_rep[:], ALU.add).then_inc(res_ready, 1)
            in_groups(pool, body)
            pool.wait_ge(out_done, (G - 1) * 16)
            accumulate(G, 0)

        @block.scalar
        def _(act):
            def split_stage(n):
                act.wait_ge(stage_in, STAGE_COUNT[n])
                lo, hi = STAGE_COLS[n]
                act.activation(w_hi[:, lo:hi], stage[:, 0:hi - lo], ACT.Copy).then_inc(stage_hi, 1)

            act.wait_ge(stage_in, STAGE_COUNT[0])
            act.activation(router[:, :, 0:E_RT], stage[:, RW:RW + C * E_RT].rearrange("p (c e) -> p c e", c=C),
                           ACT.Copy).then_inc(router_hi, 1)
            split_stage(0)

            def body(gl, ga, gf):
                def exponentials(b, q):
                    k, use = q % 2, b * (NQ // 2) + q // 2
                    act.wait_ge(st_full[k], ga * (B * NQ // 2) + use + 1)
                    if use:
                        act.wait_ge(pv_done[k], ga * (B * NQ // 2) + use)
                    elif gf is not None and LIGHT[k]:
                        act.wait_ge(acc01_done, (gf * NE + LIGHT[k]) * 2)
                    elif gf is not None:
                        wait_if(act, gf, acc01_done, gf * (NE * 2))
                    act.activation(prob[k][:], st_bank[k][:], ACT.Exp).then_inc(exp_done[k], 1)

                for s in range(NE):
                    bn, bt, bw = (in_slot(ga, s, first) for first in (NMT_SLOT, ST_SLOT, WO_SLOT))
                    if gf is not None:
                        act.wait_ge(h1_full, gf * NE + s + 1)
                        if s:
                            act.wait_ge(v_done, gf * NE + s)
                        act.activation(gate_act, h1_bank[:], ACT.Tanh, scale=0.5).then_inc(tanh_done, 1)
                        if s == 0:
                            act.wait_ge(shifted_ready, gf + 1)
                            act.activation(expo[:], shifted[:], ACT.Exp).then_inc(expo_ready, 1)
                    if gl is not None:
                        front_piece(gl, s, -1)
                    if bn is not None:
                        act.wait_ge(nmT_full, ga * B + bn + 1)
                        act.activation(neg_maxT[0:PARTS * H, bn, :], misc[1][0:PARTS * H, 0:T // 2].bitcast(BF16),
                                       ACT.Copy).then_inc(nmT_ready, 1)
                    if bt is not None:
                        exponentials(bt, 0)
                    if s == NE - 1 and ga is not None:
                        for c in range(C):
                            act.wait_ge(xn2T_full, ga * C + c + 1)
                            if gf is not None and c == 0:
                                act.wait_ge(h3_full, (gf + 1) * NE)
                            act.activation(xn2T_hi[:, c, :], turn_bank[c][:], ACT.Copy).then_inc(xn2T_hi_done, 1)
                    if bw is not None:
                        act.wait_ge(catT_full, ga * B + bw + 1)
                        act.activation(catT_hi[:], misc[1][:, 0:C * T].rearrange("p (c t) -> p c t", c=C),
                                       ACT.Copy).then_inc(catT_hi_done, 1)
                    for q in range(NQ):
                        if q and bt is not None:
                            exponentials(bt, q)
                        if gf is not None and q == (bt is not None):
                            act.wait_ge(v_done, gf * NE + s + 1)
                            act.activation(hid_hi[s % 2][:], hidden[s % 2], ACT.Copy).then_inc(hid_hi_done, 1)
                        if gl is not None:
                            front_piece(gl, s, q)
                    if bt is not None:
                        act.wait_ge(pv_done[1], (ga * B + bt + 1) * (NQ // 2))
                        act.activation(outT[:], misc[0][:], ACT.Copy).then_inc(outT_ready, 1)
                    if before_slot(gf, s):
                        take_y(gf, s, ga is None)
                    if isinstance(gl, int) and gl == 0 and s == 8:
                        split_stage(1)
                    if isinstance(ga, int) and ga == 0 and s in (HI2, HI3):
                        split_stage(2 if s == HI2 else 3)

            def take_y(gf, s, alone=False):
                e, count = before_slot(gf, s)
                gate = [1.0 if e < E_SH else gates[:, b, e - E_SH:e - E_SH + 1] for b in range(B)]
                if s in LIGHT:
                    act.wait_ge(y_full, count * 2 + 1)
                    for b in (0, 1):
                        act.activation(prob[s][:, b * D:(b + 1) * D], y_of(e, b), ACT.Copy, scale=gate[b]).then_inc(y01_taken, 1)
                act.wait_ge(y_full, count * 2 + 2)
                if e == E_SH:
                    act.wait_ge(gates_ready, gf + 1)
                if not (isinstance(gf, int) and gf == 0 and s <= 2):
                    act.wait_ge(acc23_done, count * 2 - 2)
                for b in (2, 3):
                    act.activation(y_gated[:, e % 2, b - 2, :], y_of(e, b, alone), ACT.Copy, scale=gate[b]).then_inc(y_taken, 1)

            def front_piece(gl, s, q):
                if (s, q) in SPLIT_T:
                    n = SPLIT_T[s, q]
                    dst = (xnT_hi[:, 0, :], xnT_hi[:, 1, :], cT_hi[:])[n]
                    act.wait_ge(front_full, gl * FRONT + XT0 + n + 1)
                    act.activation(dst, turned_in(gl, n)[:], ACT.Copy).then_inc(front_hi, 1)
                if (s, q) in OTHER_PARTS:
                    n = OTHER_PARTS[s, q]
                    side, m = divmod(n, 2)
                    act.wait_ge(rest_ready, gl * 4 + n + 1)
                    act.activation(parts[:, side, 1, m, :], proj[:, n % 2, :], ACT.Copy).then_inc(part2_ready, 1)
                if (s, q) in FIRST_PART:
                    n = FIRST_PART[s, q]
                    side, m = divmod(n, 2)
                    if isinstance(gl, int) and gl == 0 and n == 0:
                        act.wait_ge(const_ready, 3)
                    act.wait_ge(front_full, gl * FRONT + Q0 + n + 1)
                    if n >= 2:
                        act.wait_ge(part3_ready, gl * 4 + n - 1)
                    else:
                        wait_if(act, gl, part3_ready, gl * 4)
                    bias = (bq_quarter, bk_col)[side][:, m:m + 1]
                    act.activation(proj[:, n % 2, :], front_bank[Q0 + n][:], ACT.Identity, bias=bias,
                                   scale=(DK ** -0.5, 1.0)[side]).then_inc(proj_ready, 1)
                    wait_if(act, gl, parts_out[m], gl * (2 * PARTS * 16))
                    act.activation(parts[:, side, 0, m, :], front_bank[Q0 + n][:], ACT.Identity, bias=bias,
                                   scale=(DK ** -0.5, 1.0)[side]).then_inc(part1_ready, 1)

            in_groups(act, body)
            take_y(G, 0)

        @block.vector
        def _(dve):
            dve.wait_ge(ident_in_done, 16)
            dve.tensor_copy(ident_b[:], ident[:]).then_inc(const_ready, 1)

            def split_stage(n):
                dve.wait_ge(stage_hi, n + 1)
                lo, hi = STAGE_COLS[n]
                dve.tensor_tensor(w_lo[:, lo:hi], stage[:, 0:hi - lo], w_hi[:, lo:hi].bitcast(F32),
                                  ALU.subtract).then_inc(stage_lo, 1)

            def accumulate(gf, s):
                e, count = before_slot(gf, s)
                dve.wait_ge(y_full, count * 2 + 1)
                for b in (0, 1):
                    dve.wait_ge(acc01_done, count * 2 + b)
                    dst = src = acc[:, b, :]
                    if e < E_SH:
                        ins = dve.tensor_tensor(dst, y_of(e, b), src, ALU.add)
                    else:
                        if e == E_SH and b == 0:
                            dve.wait_ge(gates_ready, gf + 1)
                        ins = dve.scalar_tensor_tensor(out=dst, in0=y_of(e, b), scalar=gates[:, b, e - E_SH:e - E_SH + 1],
                                                       in1=src, op0=ALU.mult, op1=ALU.add)
                    ins.then_inc(acc01_done, 1)

            def body(gl, ga, gf):
                steps = {"ln": 0, "att": 0, "ffn": 0}

                def ln_step(ins, wait=True):
                    steps["ln"] += 1
                    ins.then_inc(dve_ln, 1)
                    if wait:
                        dve.wait_ge(dve_ln, gl * DVE_LN + steps["ln"])

                def att_step(ins):
                    steps["att"] += 1
                    ins.then_inc(dve_att, 1)
                    dve.wait_ge(dve_att, ga * DVE_ATT + steps["att"])

                def ffn_step(ins, wait=True):
                    steps["ffn"] += 1
                    ins.then_inc(dve_ffn, 1)
                    if wait:
                        dve.wait_ge(dve_ffn, gf * DVE_FFN + steps["ffn"])

                def row_maximum(b, q):
                    dve.wait_ge(s_full, (ga * B + b) * NQ + q + 1)
                    dve.tensor_reduce(row_max[:, b, 4 * q:4 * q + 4], score_bank(b, q)[:].rearrange("p (h t) -> p h t", h=4),
                                      AX.X, ALU.max).then_inc(s_max, 1)

                def front_piece(s, q):
                    if (s, q) in SPLIT_T:
                        n = SPLIT_T[s, q]
                        hi = (xnT_hi[:, 0, :], xnT_hi[:, 1, :], cT_hi[:])[n]
                        lo = (xnT_lo[:, 0, :], xnT_lo[:, 1, :], cT_lo[:])[n]
                        dve.wait_ge(front_hi, gl * 3 + n + 1)
                        dve.tensor_tensor(lo, turned_in(gl, n)[:], hi.bitcast(F32), ALU.subtract).then_inc(front_lo, 1)
                    if (s, q) in FIRST_PART:
                        n = FIRST_PART[s, q]
                        side, m = divmod(n, 2)
                        dve.wait_ge(proj_ready, gl * 4 + n + 1)
                        dve.wait_ge(part1_ready, gl * 4 + n + 1)
                        dve.tensor_tensor(proj[:, n % 2, :], proj[:, n % 2, :], parts[:, side, 0, m, :],
                                          ALU.subtract).then_inc(rest_ready, 1)
                    if (s, q) in TAKE_V:
                        take_v(gl, TAKE_V[s, q])

                def take_v(g, n):
                    if isinstance(g, int) and g == 0 and n == 0:
                        dve.wait_ge(pool_const, 2)
                    dve.wait_ge(front_full, g * FRONT + V01 + n + 1)
                    dve.tensor_tensor(v_aug[:, 2 * n:2 * n + 2, :, 0:DK],
                                      front_bank[V01 + n][:].rearrange("p (b h d) -> p b h d", h=H, d=DK),
                                      bv_rep[:].rearrange("p (h d) -> p h d", d=DK).unsqueeze(1).broadcast_to([128, 2, H, DK]),
                                      ALU.add).then_inc(v_ready, 1)

                def route():
                    dve.wait_ge(logits_full, gf + 1)
                    halves = misc[0][:, 0:B * 2 * E_RT].rearrange("p (b n e) -> p b n e", b=B, n=2)
                    ffn_step(dve.tensor_tensor(logits[:], halves[:, :, 0, :], rb_rep[:].unsqueeze(1).broadcast_to(
                        [128, B, E_RT]), ALU.add))
                    dve.tensor_tensor(logits[:], halves[:, :, 1, :], logits[:], ALU.add).then_inc(logits_out, 1)
                    dve.wait_ge(logits_out, gf + 1)
                    ffn_step(dve.tensor_reduce(top[:], logits[:], AX.X, ALU.max))
                    dve.tensor_tensor(shifted[:], logits[:], top[:].unsqueeze(2).broadcast_to([128, B, E_RT]),
                                      ALU.subtract).then_inc(shifted_ready, 1)

                def turn_low():
                    for c in range(C):
                        dve.wait_ge(xn2T_hi_done, ga * C + c + 1)
                        dve.tensor_tensor(xn2T_lo[:, c, :], turn_bank[c][:], xn2T_hi[:, c, :].bitcast(F32),
                                          ALU.subtract).then_inc(xn2T_lo_done, 1)

                def choose(n):
                    other = logits[:].unsqueeze(2).broadcast_to([128, B, E_RT, E_RT])
                    own = logits[:].unsqueeze(3).broadcast_to([128, B, E_RT, E_RT])
                    if n == 0:
                        dve.tensor_tensor(pair_eq[:], other, own, ALU.is_equal).then_inc(pairs_ready, 1)
                    elif n == 1:
                        dve.tensor_tensor(pair_gt[:], other, own, ALU.is_gt).then_inc(pairs_ready, 1)
                    elif n == 2:
                        dve.wait_ge(pair_before, (gf + 1) * 2)
                        ffn_step(dve.tensor_reduce(rank[:], pair_gt[:], AX.X, ALU.add), wait=False)
                    elif n == 3:
                        dve.wait_ge(dve_ffn, gf * DVE_FFN + steps["ffn"])
                        dve.wait_ge(expo_ready, gf + 1)
                        ffn_step(dve.scalar_tensor_tensor(out=chosen[:], in0=rank[:], scalar=1.5, in1=expo[:],
                                                          op0=ALU.is_lt, op1=ALU.mult), wait=False)
                    elif n == 4:
                        dve.wait_ge(dve_ffn, gf * DVE_FFN + steps["ffn"])
                        ffn_step(dve.tensor_reduce(gsum[:], chosen[:], AX.X, ALU.add), wait=False)
                    elif n == 5:
                        dve.wait_ge(dve_ffn, gf * DVE_FFN + steps["ffn"])
                        ffn_step(dve.reciprocal(grec[:], gsum[:]), wait=False)
                    else:
                        dve.wait_ge(dve_ffn, gf * DVE_FFN + steps["ffn"])
                        wait_if(dve, gf, y_taken, gf * (NE * 2))
                        dve.tensor_tensor(gates[:], chosen[:], grec[:].unsqueeze(2).broadcast_to(
                            [128, B, E_RT]), ALU.mult).then_inc(gates_ready, 1)

                def low_cat(b):
                    dve.wait_ge(catT_hi_done, ga * B + b + 1)
                    dve.tensor_tensor(catT_lo[:], misc[1][:, 0:C * T].rearrange("p (c t) -> p c t", c=C),
                                      catT_hi[:].bitcast(F32), ALU.subtract).then_inc(catT_lo_done, 1)

                for s in range(NE):
                    bs, bw = (in_slot(ga, s, first) for first in (S_SLOT, WO_SLOT))
                    bx = in_slot(ga, s, XN2_SLOT)
                    if bx is not None:
                        dve.wait_ge(dve_att, ga * DVE_ATT + steps["att"])
                    if bs:
                        row_maximum(bs, 0)
                    if gf is not None:
                        dve.wait_ge(tanh_done, gf * NE + s + 1)
                        dve.scalar_tensor_tensor(out=gate_act, in0=gate_act, scalar=1.0, in1=h1_bank[:],
                                                 op0=ALU.add, op1=ALU.mult).then_inc(u_done, 1)
                    if gf is not None and s == 0:
                        route()
                    if bx is not None:
                        dve.bn_aggr(mv2[:, bx, :], stats2[:, bx, :]).then_inc(dve_att, 1)
                        steps["att"] += 1
                        dve.wait_ge(dve_att, ga * DVE_ATT + steps["att"])
                        dve.tensor_scalar(var_eps2[:, bx:bx + 1], mv2[:, bx, 1:2], EPS, None,
                                          ALU.add).then_inc(var2_ready, 1)
                    if bw is not None:
                        tok = misc[0][:].rearrange("p (h d) -> p h d", h=H)
                        dve.wait_ge(out_tok_full, ga * B + bw + 1)
                        att_step(dve.reciprocal(rden[:], tok[:, :, DK]))
                        dve.tensor_tensor(cat[:].rearrange("p (h d) -> p h d", h=H), tok[:, :, 0:DK],
                                          rden[:].unsqueeze(2).broadcast_to([128, H, DK]), ALU.mult).then_inc(cat_ready, 1)
                    if ga is not None and s == V23_SLOT:
                        take_v(ga, 1)
                    if bs == 0:
                        row_maximum(bs, 0)
                    if bs in (0, 1):
                        row_maximum(bs, 1)
                    if gf is not None:
                        dve.wait_ge(u_done, gf * NE + s + 1)
                        dve.wait_ge(h3_full, gf * NE + s + 1)
                        if s >= 2:
                            dve.wait_ge(hid_lo_done, gf * NE + s - 1)
                        else:
                            wait_if(dve, gf, hid_lo_done, gf * NE + s - 1)
                        dve.scalar_tensor_tensor(out=hidden[s % 2], in0=gate_act, scalar=0.5, in1=h3_bank[:],
                                                 op0=ALU.mult, op1=ALU.mult).then_inc(v_done, 1)
                    if gl is not None:
                        front_piece(s, -1)
                    if bs in (2, 3):
                        row_maximum(bs, 1)
                    if s == NE - 1 and ga is not None:
                        turn_low()
                    for q in range(NQ):
                        if q == 0 and bs is None and bw is not None:
                            low_cat(bw)
                        if q in (1, 2) and bs is not None:
                            row_maximum(bs, q + 1)
                        if q == 1 and bs is not None and bw is not None:
                            low_cat(bw)
                        if q == (1 if s == 6 else 2) and bw is not None:
                            dve.wait_ge(wo_full, ga * B + bw + 1)
                            dve.wait_ge(res_ready, (ga + 1) * B)
                            if gf is not None and bw == 0:
                                dve.wait_ge(acc01_done, (gf * NE + 1) * 2)
                                dve.wait_ge(acc23_done, (gf * NE + 1) * 2)
                            dve.tensor_tensor(x2[:, bw, :], misc[1][:, 0:D], x_res[:, bw, :], ALU.add).then_inc(x2_ready, 1)
                            dve.wait_ge(x2_ready, ga * B + bw + 1)
                            dve.bn_stats(stats2[:, bw, :], x2[:, bw, :]).then_inc(dve_att, 1)
                            steps["att"] += 1
                        if q == 2 and bx is not None:
                            if bx == 0:
                                wait_if(dve, ga, xn2T_full, ga * C)
                            dve.wait_ge(rstd2_ready, ga * B + bx + 1)
                            dve.tensor_scalar(xn2[:, bx, :], x2[:, bx, :], mv2[:, bx, 0:1], rstd2[:, bx:bx + 1],
                                              ALU.subtract, ALU.mult).then_inc(xn2_ready, 1)
                        if s in ACC_FIRST and q == ACC_FIRST[s] and gf is not None:
                            accumulate(gf, s)
                        if gl is not None:
                            front_piece(s, q)
                        if q == 0 and s not in ACC_FIRST and s not in LIGHT and gf is not None:
                            accumulate(gf, s)
                        if gf is not None and (s, q) in CHOOSE:
                            choose(CHOOSE[s, q])
                    if gl is not None and s == XN_SLOT:
                        wait_if(dve, gl, part3_ready, gl * 4)
                        if gf is not None:
                            wait_if(dve, gf, out_done, gf * 16)
                        dve.wait_ge(rstd_ready, gl + 1)
                        dve.wait_ge(dve_ln, (gl + 1) * DVE_LN)
                        for b in range(B) if isinstance(gl, int) and gl == 0 else (0, 1):
                            dve.tensor_scalar(xn[:, b, :], x_in[:, b, :], mean[:, b:b + 1], rstd[:, b:b + 1],
                                              ALU.subtract, ALU.mult).then_inc(xn01_ready if b < 2 else xn23_ready, 1)
                    if isinstance(gl, int) and gl == 0 and s == XN_SLOT:
                        dve.wait_ge(router_hi, 1)
                        dve.tensor_tensor(router[:, :, E_RT:], stage[:, RW:RW + C * E_RT].rearrange("p (c e) -> p c e", c=C),
                                          router[:, :, 0:E_RT].bitcast(F32), ALU.subtract).then_inc(const_ready, 1)
                        split_stage(0)
                        dve.wait_ge(consts_in, CONST_DMAS * 16)
                        dve.tensor_scalar(bq_quarter[:], bq_col[:], DK ** -0.5, None, ALU.mult).then_inc(const_ready, 1)
                    if bs is not None:
                        nm = [neg_max[:, bs, p * H:(p + 1) * H] for p in range(PARTS)]
                        if isinstance(ga, int) and ga == 0 and bs == 0:
                            dve.wait_ge(pool_const, 3)
                        dve.wait_ge(s_max, (ga * B + bs + 1) * NQ)
                        wait_if(dve, ga, nmT_full, ga * B)
                        att_step(dve.tensor_scalar(nm[0], row_max[:, bs, :], -1.0, None, ALU.mult))
                        att_step(dve.scalar_tensor_tensor(out=max_rest[:, bs, :], in0=row_max[:, bs, :], scalar=-1.0,
                                                          in1=nm[0], op0=ALU.mult, op1=ALU.subtract))
                        att_step(dve.tensor_copy(nm[1], max_rest[:, bs, :]))
                        dve.tensor_tensor(nm[2], max_rest[:, bs, :], nm[1], ALU.subtract).then_inc(nm_ready, 1)
                    if gl is not None and s in STATS:
                        if s == min(STATS):
                            dve.wait_ge(x_loaded, (gl + 1) * 16)
                            wait_if(dve, gl, xn23_ready, gl * 2)
                        for b in STATS[s]:
                            ln_step(dve.bn_stats(stats[:, b, :], x_in[:, b, :]), wait=False)
                    if gl is not None and s == max(STATS):
                        even, odd = stats[:, :, 0:3], stats[:, :, 3:6]
                        dve.wait_ge(dve_ln, gl * DVE_LN + steps["ln"])
                        ln_step(dve.tensor_tensor(mean_parts[:, 0, :], even[:, :, 1], odd[:, :, 1], ALU.add), wait=False)
                        ln_step(dve.tensor_tensor(mean_parts[:, 1, :], even[:, :, 1], odd[:, :, 1], ALU.subtract), wait=False)
                        ln_step(dve.scalar_tensor_tensor(out=mean_parts[:, 2, :], in0=even[:, :, 2], scalar=D * EPS,
                                                         in1=odd[:, :, 2], op0=ALU.add, op1=ALU.add))
                        ln_step(dve.scalar_tensor_tensor(out=mean_parts[:, 1, :], in0=mean_parts[:, 1, :], scalar=0.25,
                                                         in1=mean_parts[:, 1, :], op0=ALU.mult, op1=ALU.mult))
                        dve.scalar_tensor_tensor(out=var_eps[:], in0=mean_parts[:, 2, :], scalar=1.0 / D,
                                                 in1=mean_parts[:, 1, :], op0=ALU.mult, op1=ALU.add).then_inc(var_ready, 1)
                        ln_step(dve.tensor_scalar(mean[:], mean_parts[:, 0, :], 0.5, None, ALU.mult))
                    if isinstance(gl, int) and gl == 0 and s == 8:
                        split_stage(1)
                assert gl is None or steps["ln"] == DVE_LN, steps
                assert ga is None or steps["att"] == DVE_ATT, steps
                assert gf is None or steps["ffn"] == DVE_FFN, steps

            in_groups(dve, body)

        @block.tensor
        def _(pe):
            def three(out_ap, terms):
                n = len(terms)
                for i, (lh, ll, rh, rl) in enumerate(terms):
                    pe.matmul(out_ap, lh, rh, start=(i == 0), stop=False)
                    pe.matmul(out_ap, ll, rh, start=False, stop=False)
                    ins = pe.matmul(out_ap, lh, rl, start=False, stop=(i == n - 1))
                return ins

            def weights(start, size):
                return w_hi[:, start:start + size], w_lo[:, start:start + size]

            def stay_warm(n):
                for _ in range(n):
                    pe.matmul(y_bank[:], neg_max[:, 0, :], neg_max[:].rearrange("p b t -> p (b t)"), start=True, stop=True)

            pe.wait_ge(pool_const, 3)
            stay_warm(WARM_START)
            pe.wait_ge(ident_in_done, 16)

            def front(gl, ga, use):
                bank = turned_in(gl, use - XT0) if use in (XT0, XT1, CT) else front_bank[use]
                first = isinstance(gl, int) and gl == 0
                if use in (XT0, XT1):
                    m = use - XT0
                    if m == 0:
                        if ga is not None:
                            pe.wait_ge(s_max, (ga + 1) * (B * NQ))
                        pe.wait_ge(xn01_ready, (gl + 1) * 2)
                        pe.wait_ge(xn23_ready, (gl + 1) * 2)
                    elif not first:
                        pe.wait_ge(front_lo, gl * 3 + 1)
                    for b in range(B):
                        ins = pe.transpose(bank[:, b * T:(b + 1) * T], xn[:, b, m * 128:(m + 1) * 128], ident[:])
                elif use == CT:
                    pe.wait_ge(c_loaded, (gl + 1) * 16)
                    if not first:
                        pe.wait_ge(front_lo, gl * 3 + 2)
                    for b in range(B):
                        ins = pe.transpose(bank[:, b * T:(b + 1) * T], c_in[:, b, :], ident[:])
                elif use in (Q0, Q1):
                    m = use - Q0
                    if isinstance(gl, int) and gl == 0 and m == 0:
                        pe.wait_ge(stage_lo, 1)
                    if m == 0:
                        pe.wait_ge(front_lo, gl * 3 + 3)
                    elif ga is not None:
                        pe.wait_ge(exp_done[0], (ga + 1) * (B * NQ // 2))
                    ins = three(bank[:], [(*weights(WQ + c * D + m * 128, 128), xnT_hi[:, c, :], xnT_lo[:, c, :])
                                          for c in range(C)])
                elif use in (K0, K1):
                    m = use - K0
                    if m == 0 and ga is not None:
                        pe.wait_ge(exp_done[1], (ga + 1) * (B * NQ // 2))
                    if m == 1:
                        pe.wait_ge(part1_ready, gl * 4 + 1)
                    ins = three(bank[:], [(*weights(WK + m * 128, 128), cT_hi[:], cT_lo[:])])
                else:
                    n = use - V01
                    if n == 0:
                        pe.wait_ge(part1_ready, gl * 4 + 2)
                    else:
                        pe.wait_ge(s_max, gl * (B * NQ) + NQ)
                    for b in (2 * n, 2 * n + 1):
                        tok = slice(b * T, (b + 1) * T)
                        ins = three(bank[:, (b % 2) * D:(b % 2 + 1) * D],
                                    [(cT_hi[:, tok], cT_lo[:, tok], *weights(WV, D))])
                ins.then_inc(front_full, 1)

            def down(gf, s, half, alone=False):
                e, count = before_slot(gf, s)
                k = e % 2
                if half == 0:
                    pe.wait_ge(hid_lo_done, count + 1)
                if half == 0:
                    if e == 0:
                        if not (isinstance(gf, int) and gf == 0):
                            pe.wait_ge(y01_taken, y01_count(gf, s))
                    elif e == 1:
                        pe.wait_ge(y01_taken, y01_count(gf, 1) + 2)
                    elif e <= SPARE_Y and not alone:
                        pe.wait_ge(y_taken, count * 2)
                    else:
                        pe.wait_ge(acc01_done, count * 2)
                elif e == 0:
                    pe.wait_ge(logits_out, gf + 1)
                elif e < SPARE_Y and not alone:
                    pe.wait_ge(acc01_done, count * 2 + 2)
                elif e > SPARE_Y or alone:
                    pe.wait_ge(y_taken, count * 2)
                for b in (2 * half, 2 * half + 1):
                    tok = slice(b * T, (b + 1) * T)
                    ins = three(y_of(e, b, alone), [(hid_hi[k][:, tok], hid_lo[k][:, tok], *weights(W2 + e * D, D))])
                ins.then_inc(y_full, 1)

            def logits_of(gf):
                for b in range(B):
                    tok = slice(b * T, (b + 1) * T)
                    both = misc[0][:, b * 2 * E_RT:(b + 1) * 2 * E_RT]
                    for c in range(C):
                        if c:
                            pe.matmul(both[:, 0:E_RT], xn2T_lo[:, c, tok], router[:, c, 0:E_RT], start=False, stop=False)
                        ins = pe.matmul(both, xn2T_hi[:, c, tok], router[:, c, :], start=(c == 0), stop=(c == C - 1))
                        if not c:
                            pe.matmul(both[:, 0:E_RT], xn2T_lo[:, c, tok], router[:, c, 0:E_RT], start=False, stop=False)
                ins.then_inc(logits_full, 1)

            def body(gl, ga, gf):
                def up(which, s):
                    bank, start = ((h1_bank, W1), (h3_bank, W3))[which]
                    if s == 0 and which == 0:
                        pe.wait_ge(stage_lo, 4)
                    if s:
                        pe.wait_ge((u_done, v_done)[which], gf * NE + s)
                    else:
                        wait_if(pe, gf, (u_done, v_done)[which], gf * NE)
                        if which == 0:
                            pe.wait_ge(xn2T_lo_done, (gf + 1) * C)
                    three(bank[:], [(*weights(start + (s * C + c) * HID, HID), xn2T_hi[:, c, :], xn2T_lo[:, c, :])
                                    for c in range(C)]).then_inc((h1_full, h3_full)[which], 1)

                def scores(b, q):
                    taken = (ga * B + b) * NQ + q
                    if b == 0 and q == 0:
                        pe.wait_ge(stack_in[0], (ga + 1) * (6 * 16))
                    elif b == 0 and q == 1:
                        pe.wait_ge(v_ready, ga * 2 + 1)
                    elif b == 0 and q == 3:
                        pass
                    elif b == 1 and q == 3:
                        pe.wait_ge(v_ready, ga * 2 + 2)
                    elif b < 2 and q % 2:
                        pe.wait_ge(s_max, taken - 3)
                    elif b < 2 or (b == 2 and q == 0):
                        if b == 0:
                            pe.wait_ge(stack_in[1], (ga + 1) * (6 * 16))
                        pe.wait_ge(s_max, taken - 1)
                    else:
                        pe.wait_ge(s_max, taken)
                    tok = slice(b * T, (b + 1) * T)
                    for j in range(4):
                        ins = pe.matmul(score_bank(b, q)[:, j * T:(j + 1) * T], q_stack[0:KD, 4 * q + j, tok],
                                        k_stack[0:KD, 4 * q + j, tok], start=True, stop=True)
                    ins.then_inc(s_full, 1)

                def scores_t(b, q):
                    k, use = q % 2, b * (NQ // 2) + q // 2
                    if q == 0:
                        if isinstance(ga, int) and ga == 0 and b == 0:
                            pe.wait_ge(pool_const, 4)
                        pe.wait_ge(nm_in[b], (ga + 1) * (PARTS * 16))
                    if use:
                        pe.wait_ge(exp_done[k], ga * (B * NQ // 2) + use)
                    else:
                        pe.wait_ge(s_max, (ga * B + 1) * NQ + 2 + 2 * k)
                    tok = slice(b * T, (b + 1) * T)
                    for j in range(4):
                        ins = pe.matmul(st_bank[k][:, j * T:(j + 1) * T], k_stack[0:KM, 4 * q + j, tok],
                                        q_stack[0:KM, 4 * q + j, tok], start=True, stop=True)
                    ins.then_inc(st_full[k], 1)

                def values(b, q):
                    k, use = q % 2, b * (NQ // 2) + q // 2
                    pe.wait_ge(exp_done[k], ga * (B * NQ // 2) + use + 1)
                    if b == 0 and q == 0:
                        pe.wait_ge(v_ready, (ga + 1) * 2)
                    if q == 0 and b == 0:
                        if gf is not None:
                            pe.wait_ge(y_taken, (gf * NE + 1) * 2)
                    elif q == 0:
                        pe.wait_ge(cat_ready, ga * B + b)
                    for j in range(4):
                        ins = pe.matmul(misc[0][j * VW:(j + 1) * VW, q * T:(q + 1) * T], v_aug[:, b, 4 * q + j, :],
                                        prob[k][:, j * T:(j + 1) * T], start=True, stop=True)
                    ins.then_inc(pv_done[k], 1)

                def turn_maximum(bn, bw):
                    pe.wait_ge(nm_ready, ga * B + bn + 1)
                    if bn == 0:
                        if gf is not None:
                            wait_if(pe, gf, y_taken, gf * (NE * 2))
                    elif bw:
                        pe.wait_ge(x2_ready, ga * B + bw)
                    else:
                        pe.wait_ge(nmT_ready, ga * B + bn)
                    if isinstance(ga, int) and ga == 0 and bn == 0:
                        pe.wait_ge(const_ready, 1)
                    pe.transpose(misc[1][:, 0:T // 2].bitcast(BF16), neg_max[:, bn, :],
                                 ident_b[:]).then_inc(nmT_full, 1)

                for s in range(NE):
                    bs, bn, bt, bw = (in_slot(ga, s, first) for first in (S_SLOT, NMT_SLOT, ST_SLOT, WO_SLOT))
                    if bs:
                        scores(bs, 0)
                    if gf is not None:
                        up(0, s)
                    if gf is not None and s == 0:
                        logits_of(gf)
                    if bw is not None:
                        pe.wait_ge(outT_ready, ga * B + bw + 1)
                        for q in range(NQ):
                            ins = pe.transpose(misc[0][:, q * T:(q + 1) * T], outT[:, q * T:(q + 1) * T], ident[:])
                        ins.then_inc(out_tok_full, 1)
                    if bs == 0:
                        scores(bs, 0)
                    if bs in (0, 1):
                        scores(bs, 1)
                    if ga is not None and s == V23_SLOT:
                        front(ga, None, V23)
                    if bn == 0:
                        turn_maximum(bn, bw)
                    if gf is not None:
                        up(1, s)
                    if bn:
                        turn_maximum(bn, bw)
                    if bs in (2, 3):
                        scores(bs, 1)
                    if bt:
                        scores_t(bt, 0)
                    if before_slot(gf, s):
                        down(gf, s, 0, ga is None)
                    if bt == 0:
                        scores_t(bt, 0)
                    if bw is not None:
                        pe.wait_ge(cat_ready, ga * B + bw + 1)
                        if bn is not None:
                            pe.wait_ge(nmT_ready, ga * B + bn + 1)
                        elif bw:
                            pe.wait_ge(x2_ready, ga * B + bw)
                        for c in range(C):
                            ins = pe.transpose(misc[1][:, c * T:(c + 1) * T], cat[:, c * 128:(c + 1) * 128], ident[:])
                        ins.then_inc(catT_full, 1)
                    for q in range(NQ):
                        if q == 1 and bs is not None:
                            scores(bs, 2)
                        if q and bt is not None:
                            scores_t(bt, q)
                        if gl is not None and (s, q) in FRONT_PE:
                            front(gl, ga, FRONT_PE[s, q])
                        if q == (1 if bt is None else 2) and bs is None and bw is not None:
                            pe.wait_ge(catT_lo_done, ga * B + bw + 1)
                            three(misc[1][:, 0:D], [(catT_hi[:, c, :], catT_lo[:, c, :], *weights(WO + c * D, D))
                                                    for c in range(C)]).then_inc(wo_full, 1)
                        if q == 2 and bs is not None and bt == 0:
                            scores(bs, 3)
                        if q == 2 and bt == 0:
                            values(bt, 0)
                        if q and bt is not None and not (q == 1 and bt == 0):
                            values(bt, q - 1)
                        if q == 2 and bs is not None and bt != 0:
                            scores(bs, 3)
                        if q == 2 and bs is not None and bw is not None:
                            pe.wait_ge(catT_lo_done, ga * B + bw + 1)
                            three(misc[1][:, 0:D], [(catT_hi[:, c, :], catT_lo[:, c, :], *weights(WO + c * D, D))
                                                    for c in range(C)]).then_inc(wo_full, 1)
                    if before_slot(gf, s):
                        if (s - 1) % NE == SPARE_Y and ga is not None:
                            pe.wait_ge(x2_ready, (ga + 1) * B)
                        down(gf, s, 1, ga is None)
                    if bt is not None:
                        values(bt, NQ - 1)
                    if ga is not None and s == TURN:
                        pe.wait_ge(xn2_ready, (ga + 1) * B)
                        if gl is not None:
                            pe.wait_ge(part1_ready, gl * 4 + 4)
                        else:
                            pe.wait_ge(s_max, (ga + 1) * (B * NQ))
                        for c in range(C):
                            for b in range(B):
                                ins = pe.transpose(turn_bank[c][:, b * T:(b + 1) * T],
                                                   xn2[:, b, c * 128:(c + 1) * 128], ident[:])
                            ins.then_inc(xn2T_full, 1)
                if isinstance(gl, int) and gl == 0:
                    stay_warm(WARM_STACKS)

            in_groups(pe, body)
            down(G, 0, 0)
            down(G, 0, 1)

_INS = ["x", "ctx_512", "L0_xattn_Wq", "L0_xattn_bq", "L0_xattn_Wk", "L0_xattn_bk", "L0_xattn_Wv", "L0_xattn_bv",
        "L0_xattn_Wo", "L0_xattn_bo", "L0_ffn_router_w", "L0_ffn_router_b", "L0_ffn_routed_w1", "L0_ffn_routed_w3",
        "L0_ffn_routed_w2", "L0_ffn_shared_w1", "L0_ffn_shared_w3", "L0_ffn_shared_w2"]


def kernel(**inputs):
    import numpy as np
    import concourse.bacc as bacc
    from concourse import mybir as mb
    from concourse.bass_utils import run_bass_kernel_spmd as run

    nc = bacc.Bacc("TRN2", target_bir_lowering=False, num_devices=1)
    arrays, args = {}, []
    given = [(name, np.ascontiguousarray(inputs[name])) for name in _INS]
    given.append(("identity", np.eye(128, dtype=np.float32)))
    lower = np.tri(E_RT, E_RT, -1, dtype=np.float32)
    given.append(("before", np.ascontiguousarray(np.broadcast_to(lower, (128, E_RT, E_RT)))))
    for name, a in given:
        arrays[f"in_{name}"] = a
        args.append(nc.dram_tensor(f"in_{name}", a.shape, mb.dt.from_np(a.dtype), kind="ExternalInput").ap())
    args.append(nc.dram_tensor("out_x", (NB, T, D), F32, kind="ExternalOutput").ap())
    build(nc, *args)
    r = run(nc, [arrays], core_ids=[0])
    return r.results[0]["out_x"]
```
